# Optimizing a Trainium2 kernel written in Bass

```python
import numpy as np
import jax
import jax.numpy as jnp

def _softmax(x, axis=-1):
    return jax.nn.softmax(x, axis=axis)
def _gelu(x):
    return jax.nn.gelu(x, approximate=True)
def _silu(x):
    return jax.nn.silu(x)
def _sigmoid(x):
    return jax.nn.sigmoid(x)
def _layernorm(x, axis=-1, eps=1e-5):
    m = jnp.mean(x, axis=axis, keepdims=True)
    v = jnp.var(x, axis=axis, keepdims=True)
    return (x - m) / jnp.sqrt(v + eps)
def _scatter_add(tgt, idx, src, axis=0):
    return tgt.at[idx].add(src)
def _segment_sum(src, seg, n):
    return jax.ops.segment_sum(src, seg, n)

kernel_name = 'mk_conv_preact_d2_conv_nchw384_ac6828'

def setup_inputs(seed: int = 0):
    np.random.seed(seed)
    _w = jnp.asarray
    def _rec_inputs():
        import jax
        import jax.numpy as jnp
        _gk = jax.random.key(seed)
        x = -0.0001538 + 1 * jax.random.normal(jax.random.fold_in(_gk, 1), (4, 384, 64, 64), jnp.float32)
        return x
    x = _rec_inputs()
    def _L0_conv_setup():
        import jax, jax.numpy as jnp
        import numpy as np
        DIM = 384
        D_STATE = 16
        D_CONV = 4
        EXPAND = 2
        D_INNER = EXPAND * DIM
        DT_RANK = DIM // 16
        B_SZ, H_SP, W_SP = (4, 64, 64)

        def _silu(v):
            return v * jax.nn.sigmoid(v)
        key = jax.random.key(seed)
        ks = jax.random.split(key, 12)
        s = lambda k, shape, scale: jax.random.normal(k, shape, dtype=jnp.float32) * scale
        x = jax.random.normal(ks[0], (B_SZ, DIM, H_SP, W_SP), dtype=jnp.float32)
        inputs = {'x': x, 'ln_w': jnp.ones((DIM,), jnp.float32), 'ln_b': jnp.zeros((DIM,), jnp.float32), 'in_proj_w': s(ks[1], (2 * D_INNER, DIM), DIM ** (-0.5)), 'conv_w': s(ks[2], (D_INNER, 1, D_CONV), D_CONV ** (-0.5)), 'conv_b': s(ks[3], (D_INNER,), 0.02), 'x_proj_w': s(ks[4], (DT_RANK + 2 * D_STATE, D_INNER), D_INNER ** (-0.5)), 'dt_w': s(ks[5], (D_INNER, DT_RANK), DT_RANK ** (-0.5)), 'dt_b': s(ks[6], (D_INNER,), 0.5) - 4.0, 'A_log': jnp.log(jnp.broadcast_to(jnp.arange(1, D_STATE + 1, dtype=jnp.float32), (D_INNER, D_STATE))), 'D': jnp.ones((D_INNER,), jnp.float32), 'out_proj_w': s(ks[7], (DIM, D_INNER), D_INNER ** (-0.5))}
        return inputs
    _L0_conv_all = _L0_conv_setup()
    _L0_conv_in = {k: v for k, v in _L0_conv_all.items() if k in ('ln_w', 'ln_b', 'in_proj_w', 'conv_w', 'conv_b', 'x_proj_w', 'dt_w', 'dt_b', 'A_log', 'D', 'out_proj_w', )}
    del _L0_conv_all

    def _L1_conv_setup():
        import jax, jax.numpy as jnp
        import numpy as np
        NUM_HEADS = 8
        CHUNK = 64
        key = jax.random.key(seed)
        k1, k2, k3, k4 = jax.random.split(key, 4)
        B, C, H, W = (16, 384, 64, 64)
        x = jax.random.normal(k1, (B, C, H, W), dtype=jnp.float32)
        qkv_w = jax.random.normal(k2, (3 * C, C), dtype=jnp.float32) * C ** (-0.5)
        proj_w = jax.random.normal(k3, (C, C), dtype=jnp.float32) * C ** (-0.5)
        proj_b = jax.random.normal(k4, (C,), dtype=jnp.float32) * 0.02
        return {'x': x, 'qkv_w': qkv_w, 'proj_w': proj_w, 'proj_b': proj_b}
    _L1_conv_all = _L1_conv_setup()
    _L1_conv_in = {k: v for k, v in _L1_conv_all.items() if k in ('qkv_w', 'proj_w', 'proj_b', )}
    del _L1_conv_all

    return {
        "x": x,
        "L0_conv_ln_w": _L0_conv_in["ln_w"],
        "L0_conv_ln_b": _L0_conv_in["ln_b"],
        "L0_conv_in_proj_w": _L0_conv_in["in_proj_w"],
        "L0_conv_conv_w": _L0_conv_in["conv_w"],
        "L0_conv_conv_b": _L0_conv_in["conv_b"],
        "L0_conv_x_proj_w": _L0_conv_in["x_proj_w"],
        "L0_conv_dt_w": _L0_conv_in["dt_w"],
        "L0_conv_dt_b": _L0_conv_in["dt_b"],
        "L0_conv_A_log": _L0_conv_in["A_log"],
        "L0_conv_D": _L0_conv_in["D"],
        "L0_conv_out_proj_w": _L0_conv_in["out_proj_w"],
        "L1_conv_qkv_w": _L1_conv_in["qkv_w"],
        "L1_conv_proj_w": _L1_conv_in["proj_w"],
        "L1_conv_proj_b": _L1_conv_in["proj_b"],
    }

def reference(x, L0_conv_ln_w, L0_conv_ln_b, L0_conv_in_proj_w, L0_conv_conv_w, L0_conv_conv_b, L0_conv_x_proj_w, L0_conv_dt_w, L0_conv_dt_b, L0_conv_A_log, L0_conv_D, L0_conv_out_proj_w, L1_conv_qkv_w, L1_conv_proj_w, L1_conv_proj_b):
    import jax
    import jax.numpy as jnp
    def _L0_conv_ref(x, ln_w, ln_b, in_proj_w, conv_w, conv_b, x_proj_w, dt_w, dt_b, A_log, D, out_proj_w):
        import jax, jax.numpy as jnp
        import numpy as np
        DIM = 384
        D_STATE = 16
        D_CONV = 4
        EXPAND = 2
        D_INNER = EXPAND * DIM
        DT_RANK = DIM // 16
        B_SZ, H_SP, W_SP = (4, 64, 64)

        def _silu(v):
            return v * jax.nn.sigmoid(v)
        B, C, H, W = x.shape
        L = H * W
        xs = x.reshape(B, C, L).transpose(0, 2, 1)
        mu = jnp.mean(xs, axis=-1, keepdims=True)
        var = jnp.mean((xs - mu) ** 2, axis=-1, keepdims=True)
        xn = (xs - mu) * jax.lax.rsqrt(var + 1e-05) * ln_w + ln_b
        xz = jnp.einsum('blc,dc->bld', xn, in_proj_w)
        xb, z = jnp.split(xz, 2, axis=-1)
        xb_t = xb.transpose(0, 2, 1)
        xc = jax.lax.conv_general_dilated(xb_t, conv_w, window_strides=(1,), padding=[(D_CONV - 1, 0)], feature_group_count=D_INNER, dimension_numbers=('NCH', 'OIH', 'NCH'))
        xc = _silu(xc + conv_b[None, :, None]).transpose(0, 2, 1)
        x_dbl = jnp.einsum('bld,ed->ble', xc, x_proj_w)
        dt = x_dbl[..., :DT_RANK]
        Bm = x_dbl[..., DT_RANK:DT_RANK + D_STATE]
        Cm = x_dbl[..., DT_RANK + D_STATE:]
        dt = jax.nn.softplus(jnp.einsum('blr,dr->bld', dt, dt_w) + dt_b)
        A = -jnp.exp(A_log)

        def step(h, inp):
            dt_t, B_t, C_t, x_t = inp
            dA = jnp.exp(dt_t[:, :, None] * A[None])
            dBx = (dt_t * x_t)[:, :, None] * B_t[:, None, :]
            h = dA * h + dBx
            y_t = jnp.einsum('bdn,bn->bd', h, C_t)
            return (h, y_t)
        h0 = jnp.zeros((B, D_INNER, D_STATE), xc.dtype)
        seq = (jnp.moveaxis(dt, 1, 0), jnp.moveaxis(Bm, 1, 0), jnp.moveaxis(Cm, 1, 0), jnp.moveaxis(xc, 1, 0))
        _, ys = jax.lax.scan(step, h0, seq)
        y = jnp.moveaxis(ys, 0, 1) + xc * D
        y = y * _silu(z)
        out = jnp.einsum('bld,cd->blc', y, out_proj_w)
        return out.transpose(0, 2, 1).reshape(B, C, H, W)

    def _L1_conv_ref(x, qkv_w, proj_w, proj_b):
        import jax, jax.numpy as jnp
        import numpy as np
        NUM_HEADS = 8
        CHUNK = 64
        B, C, H, W = x.shape
        N = H * W
        nh = NUM_HEADS
        hd = C // nh
        scale = hd ** (-0.5)
        nc = N // CHUNK
        t = x.reshape(B, C, N).transpose(0, 2, 1)
        qkv = t @ qkv_w.T
        qkv = qkv.reshape(B, N, 3, nh, hd).transpose(2, 0, 3, 1, 4)
        q, k, v = (qkv[0], qkv[1], qkv[2])
        q = q.reshape(B, nh, nc, CHUNK, hd)
        k = k.reshape(B, nh, nc, CHUNK, hd)
        v = v.reshape(B, nh, nc, CHUNK, hd)
        scores = jnp.einsum('bhnqd,bhnkd->bhnqk', q, k) * scale
        attn = jax.nn.softmax(scores, axis=-1)
        out = jnp.einsum('bhnqk,bhnkd->bhnqd', attn, v)
        out = out.reshape(B, nh, N, hd).transpose(0, 2, 1, 3).reshape(B, N, C)
        out = out @ proj_w.T + proj_b
        return out.transpose(0, 2, 1).reshape(B, C, H, W)

    def _gn(v, G=32, eps=1e-5):
        B_, C_, H_, W_ = v.shape
        g = v.reshape(B_, G, C_ // G, H_, W_)
        m = jnp.mean(g, axis=(2, 3, 4), keepdims=True)
        s = jnp.var(g, axis=(2, 3, 4), keepdims=True)
        return ((g - m) / jnp.sqrt(s + eps)).reshape(v.shape)

    def _ln_c(v, eps=1e-6):
        m = jnp.mean(v, axis=1, keepdims=True)
        s = jnp.var(v, axis=1, keepdims=True)
        return (v - m) / jnp.sqrt(s + eps)

    def _ln_t(v, eps=1e-5):
        m = jnp.mean(v, axis=-1, keepdims=True)
        s = jnp.var(v, axis=-1, keepdims=True)
        return (v - m) / jnp.sqrt(s + eps)

    def _to_tokens(v):
        B_, C_, H_, W_ = v.shape
        return v.reshape(B_, C_, H_ * W_).transpose(0, 2, 1)
    def _from_tokens(t, like):
        B_, C_, H_, W_ = like.shape
        return t.transpose(0, 2, 1).reshape(B_, C_, H_, W_)

    x = x + _L0_conv_ref(_gn(x), L0_conv_ln_w, L0_conv_ln_b, L0_conv_in_proj_w, L0_conv_conv_w, L0_conv_conv_b, L0_conv_x_proj_w, L0_conv_dt_w, L0_conv_dt_b, L0_conv_A_log, L0_conv_D, L0_conv_out_proj_w)
    x = x + _L1_conv_ref(_gn(x), L1_conv_qkv_w, L1_conv_proj_w, L1_conv_proj_b)
    return x


_drawn_inputs = setup_inputs


def setup_inputs(seed=0):
    import zlib

    import numpy as np

    out = dict(_drawn_inputs(seed))
    spreads = {'L0_conv_ln_w': (1.0, 0.2), 'L0_conv_ln_b': (0.0, 0.1), 'L0_conv_D': (1.0, 0.6)}
    factors = {'L0_conv_conv_b': 6.926,
     'L0_conv_dt_b': 26.768,
     'L1_conv_proj_b': 27.816,
     'L0_conv_x_proj_w': 8.0,
     'L0_conv_dt_w': 8.0,
     'L0_conv_A_log': 8.0,
     'L1_conv_qkv_w': 8.0,
     'L1_conv_proj_w': 8.0}
    for name, (base, spread) in spreads.items():
        noise = np.random.default_rng([zlib.crc32(name.encode()), seed]).standard_normal(out[name].shape)
        drawn = base * np.exp(spread * noise) if base else spread * noise
        out[name] = jnp.asarray(drawn.astype(out[name].dtype))
    for name, factor in factors.items():
        out[name] = (out[name] * factor).astype(out[name].dtype)
    return out
```

```python
from contextlib import ExitStack

import numpy as np

import concourse.bass as bass
from concourse import mybir

F32 = mybir.dt.float32
ALU = mybir.AluOpType
ACT = mybir.ActivationFunctionType
AX = mybir.AxisListType

P = 128
NBATCH, DIM, L = 4, 384, 4096
NJ = DIM // P
CH = 512
CPB = L // CH
NCH = NBATCH * CPB
DIN = 2 * DIM
ND = DIN // P
NS = 16
RANK = DIM // 16
NT = CH // P
HALO = 3
GROUP_PARTS = 4
HEADS, HD, WIN = 8, DIM // 8, 64
HP = 64
NU = HEADS // 2

BY_POOL = (2, 5, 8, 11)
BY_DVE = tuple(n for n in range(NS) if n not in BY_POOL)
NDV, NPL = len(BY_DVE), len(BY_POOL)
RH = 4
RC = 8

MEAN_AT, CENTRE_AT, OUT_AT, VAR_AT, NORM_AT = 5, 7, 7, NS + 4, NS + 9
IN_AT, IN_STEP = 2 * NS - 4, 3
CONV_AT = IN_AT + 4
X_AT = IN_AT + 12 * IN_STEP + 7

EXP_LN = "natural_log_exp_and_others"

C_SCAN, C_HCV, C_HCF, C_DBX, C_EXP, C_U, C_RES, C_JIT, C_ONE = 4, 4, RC, NS, NS, 1, NJ, 12, 1
C_ATT = 8


def build(nc, x, ln_w, ln_b, w_in, conv_w, conv_b, w_x, w_dt, dt_b, a_log, d_skip, w_out,
          w_q, w_k, w_v, w_p, proj_b, out):
    xc_d = nc.dram_tensor("xc_spill", (NCH + 1, P, ND, CH), F32).ap()
    z_d = nc.dram_tensor("z_spill", (NCH + 1, P, ND, CH), F32).ap()
    bc_d = nc.dram_tensor("bc_spill", (NCH + 1, 2 * NS, CH), F32).ap()
    x1_d = nc.dram_tensor("x1", (NCH + 1, P, NJ, CH), F32).ap()
    with ExitStack() as ctx:
        ident = ctx.enter_context(nc.sbuf_tensor("ident", [P, P], F32))
        quarter = ctx.enter_context(nc.sbuf_tensor("quarter", [P, P], F32))
        mean_w = ctx.enter_context(nc.sbuf_tensor("mean_w", [P, P], F32))
        eps_col = ctx.enter_context(nc.sbuf_tensor("eps_col", [P, 1], F32))
        stats = ctx.enter_context(nc.sbuf_tensor("stats", [P, (NCH + 1) * NJ * 6], F32))
        gsc = ctx.enter_context(nc.sbuf_tensor("gsc", [P, NCH], F32))
        gbi = ctx.enter_context(nc.sbuf_tensor("gbi", [P, NCH], F32))
        input_statistics(nc, x, ident, quarter, mean_w, eps_col, stats)
        group_affine(nc, "in", stats, quarter, eps_col, gsc, gbi)
        scan_layer(nc, x, ln_w, ln_b, w_in, conv_w, conv_b, w_x, w_dt, dt_b, a_log, d_skip, w_out,
                   xc_d, z_d, bc_d, x1_d, ident, mean_w, eps_col, stats, gsc, gbi)
        group_affine(nc, "mid", stats, quarter, eps_col, gsc, gbi)
        attention_layer(nc, x1_d, w_q, w_k, w_v, w_p, proj_b, out, ident, gsc, gbi)


def input_statistics(nc, x, ident, quarter, mean_w, eps_col, stats):
    RX = 4
    with ExitStack() as ctx:
        xt = ctx.enter_context(nc.sbuf_tensor("st_x", [P, RX, NJ, CH], F32))
        loaded = [ctx.enter_context(nc.semaphore(f"st_loaded{r}")) for r in range(RX)]
        done = ctx.enter_context(nc.semaphore("st_done"))
        made = ctx.enter_context(nc.semaphore("st_made"))
        block = ctx.enter_context(nc.Block())

        @block.sync
        def _(sp):
            with sp.Fori(0, NCH // RX) as g:
                for r in range(RX):
                    sp.wait_ge(done, g * (RX * NJ) + (r + 1) * NJ)
                    sp.dma_start(xt[:, r], x[g * RX + r]).then_inc(loaded[r], 16)

        @block.vector
        def _(dve):
            dve.sem_inc(done, RX * NJ)
            nc.vector.memset(stats[:, 0:NJ * 6], 0.0)
            nc.vector.memset(eps_col[:], 1e-5)
            nc.vector.memset(mean_w[:], 1.0 / DIM)
            with dve.Fori(0, NCH // RX) as g:
                for r in range(RX):
                    dve.wait_ge(loaded[r], g * 16 + 16)
                    for j in range(NJ):
                        at = (g * RX + (r + 1)) * (NJ * 6) + j * 6
                        nc.vector.bn_stats(stats[:, bass.ds(at, 6)], xt[:, r, j, :]).then_inc(done, 1)

        @block.gpsimd
        def _(pool):
            nc.gpsimd.memset(ident[:], 0.0).then_inc(made, 1)
            nc.gpsimd.memset(quarter[:], 1.0 / GROUP_PARTS).then_inc(made, 1)
            pool.wait_ge(made, 2)
            nc.gpsimd.affine_select(out=ident[:], in_=ident[:], compare_op=ALU.not_equal, fill=1.0,
                                    base=0, pattern=[[-1, P]], channel_multiplier=1).then_inc(made, 1)
            v = quarter[:].rearrange("p (g k) -> p g k", k=GROUP_PARTS)
            nc.gpsimd.affine_select(out=v, in_=v, compare_op=ALU.is_ge, fill=0.0, base=0,
                                    pattern=[[-GROUP_PARTS, P // GROUP_PARTS], [0, GROUP_PARTS]],
                                    channel_multiplier=1).then_inc(made, 1)
            pool.wait_ge(made, 4)
            nc.gpsimd.affine_select(out=v, in_=v, compare_op=ALU.is_ge, fill=0.0, base=GROUP_PARTS - 1,
                                    pattern=[[GROUP_PARTS, P // GROUP_PARTS], [0, GROUP_PARTS]],
                                    channel_multiplier=-1).then_inc(made, 1)
            pool.wait_ge(made, 5)


def group_affine(nc, tag, stats, quarter, eps_col, gsc, gbi):
    with ExitStack() as ctx:
        mv = ctx.enter_context(nc.sbuf_tensor(f"{tag}_mv", [P, NBATCH, 2], F32))
        dev = ctx.enter_context(nc.sbuf_tensor(f"{tag}_dev", [P, NBATCH], F32))
        sq = ctx.enter_context(nc.sbuf_tensor(f"{tag}_sq", [P, NBATCH], F32))
        mean = ctx.enter_context(nc.sbuf_tensor(f"{tag}_mean", [P, NBATCH], F32))
        rs = ctx.enter_context(nc.sbuf_tensor(f"{tag}_rs", [P, NBATCH], F32))
        bi = ctx.enter_context(nc.sbuf_tensor(f"{tag}_bi", [P, NBATCH], F32))
        pm = ctx.enter_context(nc.psum_tensor(f"{tag}_pm", [P, 512], F32))
        pv = ctx.enter_context(nc.psum_tensor(f"{tag}_pv", [P, 512], F32))
        dv = ctx.enter_context(nc.semaphore(f"{tag}_dv"))
        mm = ctx.enter_context(nc.semaphore(f"{tag}_mm"))
        ac = ctx.enter_context(nc.semaphore(f"{tag}_ac"))
        block = ctx.enter_context(nc.Block())

        @block.vector
        def _(dve):
            per = CPB * NJ * 6
            for b in range(NBATCH):
                s = stats[:, NJ * 6 + b * per:NJ * 6 + (b + 1) * per]
                nc.vector.bn_aggr(mv[:, b, :], s).then_inc(dv, 1)
            dve.wait_ge(dv, 4)
            nc.vector.tensor_copy(mean[:], mv[:, :, 0]).then_inc(dv, 1)
            dve.wait_ge(mm, 1)
            nc.vector.tensor_tensor(dev[:], mv[:, :, 0], pm[:, 0:NBATCH], ALU.subtract).then_inc(dv, 1)
            dve.wait_ge(dv, 6)
            nc.vector.tensor_tensor(sq[:], dev[:], dev[:], ALU.mult).then_inc(dv, 1)
            dve.wait_ge(dv, 7)
            nc.vector.tensor_tensor(sq[:], sq[:], mv[:, :, 1], ALU.add).then_inc(dv, 1)
            dve.wait_ge(ac, 2)
            nc.vector.scalar_tensor_tensor(out=bi[:], in0=pm[:, 0:NBATCH], scalar=-1.0, in1=rs[:],
                                           op0=ALU.mult, op1=ALU.mult).then_inc(dv, 1)
            dve.wait_ge(dv, 9)
            for dst, src in ((gsc, rs), (gbi, bi)):
                wide = src[:].rearrange("p (b o) -> p b o", o=1).to_broadcast([P, NBATCH, CPB])
                nc.vector.tensor_copy(dst[:].rearrange("p (b c) -> p b c", c=CPB), wide).then_inc(dv, 1)
            dve.wait_ge(dv, 11)

        @block.tensor
        def _(pe):
            pe.wait_ge(dv, 5)
            nc.tensor.matmul(pm[:, 0:NBATCH], quarter[:], mean[:], start=True, stop=True).then_inc(mm, 1)
            pe.wait_ge(dv, 8)
            nc.tensor.matmul(pv[:, 0:NBATCH], quarter[:], sq[:], start=True, stop=True).then_inc(mm, 1)

        @block.scalar
        def _(act):
            act.preload_act_table_set(EXP_LN)
            act.wait_ge(mm, 2)
            nc.scalar.activation(rs[:], pv[:, 0:NBATCH], ACT.Ln, bias=eps_col[:, 0:1]).then_inc(ac, 1)
            act.wait_ge(ac, 1)
            nc.scalar.activation(rs[:], rs[:], ACT.Exp, scale=-0.5).then_inc(ac, 1)
            act.wait_ge(ac, 2)


def scan_layer(nc, x, ln_w, ln_b, w_in, conv_w, conv_b, w_x, w_dt, dt_b, a_log, d_skip, w_out,
               xc_d, z_d, bc_d, x1_d, ident, mean_w, eps_col, stats, gsc, gbi):
    with ExitStack() as ctx:
        def sb(name, shape):
            return ctx.enter_context(nc.sbuf_tensor(name, shape, F32))

        def sem(name):
            return ctx.enter_context(nc.semaphore(name))

        win = sb("win", [P, NJ, 2 * DIN])
        wx = sb("wx", [P, ND, 64])
        wdt = sb("wdt", [RANK, DIN])
        wout = sb("wout", [P, ND, NJ, P])
        cw = sb("cw", [P, ND, HALO + 1])
        cb = sb("cb", [P, ND])
        dtb = sb("dtb", [P, ND])
        dsk = sb("dsk", [P, ND])
        neg_a = sb("neg_a", [P, ND, NS])
        lnw = sb("lnw", [P, NJ])
        lnb = sb("lnb", [P, NJ])
        in_b = sb("in_b", [P, 2 * ND])
        xs = sb("xs", [P, NJ, CH])
        xn = sb("xn", [P, NJ, CH])
        xb = sb("xb", [P, 2, HALO + CH])
        halo = sb("halo", [P, ND, HALO])
        xc = sb("xc", [P, ND, CH])
        zt = sb("zt", [P, 2, CH])
        rstd = zt[:, 0, :]
        squares = [zt[:, 0, :], zt[:, 1, :], xb[:, 0, 0:CH]]
        xd = sb("xd", [64, CH])
        sp_e = sb("sp_e", [P, CH])
        sp_l = sb("sp_l", [P, CH])
        sp_w = sb("sp_w", [P, CH])
        sp_r = sb("sp_r", [P, CH])
        dt = sb("dt", [P, 2, CH])
        u = sb("u", [P, 2, CH])
        xj = sb("xj", [P, 2, CH])
        zj = sb("zj", [P, 2, CH])
        dx = sb("dx", [P, CH])
        bb = sb("bb", [P, NS, CH])
        cc = sb("cc", [P, NS, CH])
        dbx = sb("dbx", [P, RH, CH])
        h = sb("h", [P, RH, CH])
        hc = sb("hc", [P, RC, CH])
        state = sb("state", [P, ND, NS])
        yt_s = sb("yt_s", [P, CH])
        yg = sb("yg", [P, ND, CH])

        def bank(name):
            return ctx.enter_context(nc.psum_tensor(name, [P, 512], F32))

        p_da = [bank("p_da0"), bank("p_da1")]
        p_yt = [bank("p_yt0"), bank("p_yt1")]
        p_yb = bank("p_yb")
        p_dt = bank("p_dt")
        p_g = [bank("p_g0"), bank("p_g1")]

        s_w = sem("weights_loaded")
        s_prep = sem("prepared")
        s_prepa = sem("prepared_act")
        s_prepm = sem("prepared_pe")
        s_exp = sem("exp_done")
        s_scan = sem("scan_done")
        s_hcv = sem("hc_dve")
        s_hcg = sem("hc_pool")
        s_hcf = sem("hc_used")
        s_state = sem("state_kept")
        s_dbx = sem("dbx_done")
        s_u = sem("u_done")
        s_jit = sem("softplus_act")
        s_dt = sem("softplus_dve")
        s_re = sem("softplus_pool")
        s_dtm = sem("dt_mm")
        s_dxu = sem("dx_used")
        s_yts = sem("yt_copied")
        s_yb = sem("yb_done")
        s_gate = sem("gated")
        s_om = sem("out_mm")
        s_res = sem("residual_done")
        s_stat = sem("stats_done")
        s_lna = sem("ln_act")
        s_lnm = sem("ln_mm")
        s_lnd = sem("ln_dve")
        s_im = sem("in_mm")
        s_iev = sem("in_copied")
        s_cv = sem("conv_done")
        s_si = sem("silu_done")
        s_xm = sem("x_mm")
        s_xd = sem("xd_done")
        s_rl = sem("residual_loaded")
        s_xl = sem("x_loaded")
        s_os = sem("x1_stored")
        s_xcs = [sem(f"xc_stored{k}") for k in range(3)]
        s_zs = [sem(f"z_stored{k}") for k in range(3)]
        s_bcs = sem("bc_stored")
        s_bl = [sem(f"b_loaded{q}") for q in range(4)]
        s_cl = [sem(f"c_loaded{q}") for q in range(4)]
        s_xjl = [sem("xj_loaded0"), sem("xj_loaded1")]
        s_zjl = [sem("zj_loaded0"), sem("zj_loaded1")]

        block = ctx.enter_context(nc.Block())
        N_LOADS = 12

        def in_tile(k):
            return 2 * (k // 4) + k % 2, k % 4 >= 2

        def chunks(eng, body):
            with eng.Fori(0, NBATCH) as b:
                body(b * CPB, "image", b)
                with eng.Fori(0, CPB - 1) as c:
                    body(b * CPB + c, "chunk", b)
                body(b * CPB + (CPB - 1), "last", b)

        @block.sync
        def _(sp):
            for dst, src in ((win, w_in), (wx, w_x), (wdt, w_dt), (wout, w_out), (cw, conv_w), (cb, conv_b),
                             (dtb, dt_b), (dsk, d_skip), (neg_a, a_log), (lnw, ln_w), (lnb, ln_b)):
                sp.dma_start(dst[:], src).then_inc(s_w, 16)
            for s in s_zjl:
                sp.sem_inc(s, C_ONE)

            def load_x(q, at):
                sp.wait_ge(s_lnd, q * 6)
                sp.dma_start(xs[:], x[at]).then_inc(s_xl, 16)

            def store_silu(q, k):
                sp.wait_ge(s_si, q * 9 + 3 * k + 3)
                sp.dma_start(xc_d[q, :, 2 * k:2 * k + 2, :], xc[:, 2 * k:2 * k + 2, :]).then_inc(s_xcs[k], 16)
                sp.dma_start(z_d[q, :, 2 * k:2 * k + 2, :], zt[:]).then_inc(s_zs[k], 16)

            def store_bc(q):
                sp.wait_ge(s_xd, q + 1)
                sp.dma_start(bc_d[q], xd[32:64, :]).then_inc(s_bcs, 16)

            def load_b(q, k):
                src = bc_d[q, 4 * k:4 * k + 4, :].rearrange("(o n) t -> o n t", o=1).to_broadcast([P, 4, CH])
                sp.dma_start(bb[:, 4 * k:4 * k + 4, :], src).then_inc(s_bl[k], 16)

            def load_c(q, k):
                src = bc_d[q, NS + 4 * k:NS + 4 * k + 4, :].rearrange("(o n) t -> o n t", o=1).to_broadcast([P, 4, CH])
                sp.dma_start(cc[:, 4 * k:4 * k + 4, :], src).then_inc(s_cl[k], 16)

            def load_xj(i, d):
                m, r = i * ND + d, d % 2
                sp.compute_val(m * 6 - 8 + C_JIT)
                sp.compute_val(m)
                sp.compute_val(i * 16 + 16)
                sp.wait_ge(s_jit, m * 6 - 8 + C_JIT)
                sp.wait_ge(s_u, m)
                if d % 2 == 0:
                    sp.wait_ge(s_xcs[d // 2], i * 16 + 16)
                sp.dma_start(xj[:, r, :], xc_d[i, :, d, :]).then_inc(s_xjl[r], 16)

            def load_zj(i, d):
                m, r = i * ND + d, d % 2
                sp.compute_val(m + C_ONE)
                sp.compute_val(i * 16 + 16)
                sp.wait_ge(s_gate, m + C_ONE)
                if d % 2 == 0:
                    sp.wait_ge(s_zs[d // 2], i * 16 + 16)
                sp.dma_start(zj[:, r, :], z_d[i, :, d, :]).then_inc(s_zjl[r], 16)

            sp.dma_start(xs[:], x[0]).then_inc(s_xl, 16)
            load_x(1, 1)
            for k in range(3):
                store_silu(0, k)
            store_bc(0)
            sp.wait_ge(s_bcs, 16)
            sp.wait_ge(s_xcs[0], 16)
            sp.wait_ge(s_zs[0], 16)
            for k in range(4):
                load_b(0, k)
                load_c(0, k)
            sp.dma_start(xj[:, 0, :], xc_d[0, :, 0, :]).then_inc(s_xjl[0], 16)
            sp.dma_start(zj[:, 0, :], z_d[0, :, 0, :]).then_inc(s_zjl[0], 16)

            def body(i, kind, b):
                if kind == "image":
                    return
                q = i + 1
                for d in range(ND):
                    if d < ND - 1:
                        load_xj(i, d + 1)
                    else:
                        load_xj(q, 0)
                    if d == 0:
                        sp.wait_ge(s_im, i * 12 + 12)
                        sp.dma_start(xn[:], x[(i + (NCH - 1)) % NCH]).then_inc(s_rl, 16)
                    if d == 1:
                        sp.wait_ge(s_stat, i * NJ + NJ)
                        sp.dma_start(x1_d[i], xn[:]).then_inc(s_os, 16)
                    if d == 2:
                        load_x(q + 1, (q + 1) % NCH)
                    if d < ND - 1:
                        load_zj(i, d + 1)
                    if 2 <= d < 5:
                        store_silu(q, d - 2)
                    if d == 5:
                        store_bc(q)
                        load_zj(q, 0)
                        sp.wait_ge(s_bcs, q * 16 + 16)
                        for k in range(4):
                            e = i * (ND * NS) + 5 * NS + 4 * k + 4
                            sp.wait_ge(s_dbx, e + C_DBX)
                            load_b(q, k)
                            v = i * (ND * NDV) + 5 * NDV + sum(n < 4 * k + 4 for n in BY_DVE) + C_HCV
                            g = i * (ND * NPL) + 5 * NPL + sum(n < 4 * k + 4 for n in BY_POOL)
                            sp.compute_val(v)
                            sp.compute_val(g)
                            sp.wait_ge(s_hcv, v)
                            sp.wait_ge(s_hcg, g)
                            load_c(q, k)

            chunks(sp, body)
            sp.wait_ge(s_im, NCH * 12 + 12)
            sp.dma_start(xn[:], x[NCH - 1]).then_inc(s_rl, 16)
            sp.wait_ge(s_stat, NCH * NJ + NJ)
            sp.dma_start(x1_d[NCH], xn[:]).then_inc(s_os, 16)
            sp.wait_ge(s_xl, (NCH + 2) * 16)
            sp.wait_ge(s_os, (NCH + 1) * 16)
            for s in s_xcs + s_zs + s_bl + s_cl:
                sp.wait_ge(s, (NCH + 1) * 16)
            sp.wait_ge(s_xjl[0], (NCH * 3 + 1) * 16)
            sp.wait_ge(s_zjl[0], (NCH * 3 + 1) * 16 + C_ONE)

        @block.scalar
        def _(act):
            act.sem_inc(s_exp, C_EXP)
            act.sem_inc(s_jit, C_JIT)
            act.sem_inc(s_yts, C_ONE)
            act.preload_act_table_set(EXP_LN)
            act.wait_ge(s_w, 16 * 11)
            nc.scalar.activation(neg_a[:], neg_a[:], ACT.Exp).then_inc(s_prepa, 1)
            act.wait_ge(s_prepm, 1)
            nc.scalar.activation(in_b[:], p_dt[:, 0:2 * ND], ACT.Copy).then_inc(s_prepa, 1)
            act.wait_ge(s_prepa, 2)
            act.wait_ge(s_prep, 8)

            def scale(q, j):
                if j == 0:
                    act.wait_ge(s_xl, q * 16 + 16)
                    act.wait_ge(s_prep, 8)
                at = bass.ds(q % NCH, 1)
                nc.scalar.activation(xs[:, j, :], xs[:, j, :], ACT.Identity, scale=gsc[:, at],
                                     bias=gbi[:, at]).then_inc(s_lna, 1)

            def square(q, j):
                act.wait_ge(s_lnd, q * 6 + j + 1)
                if j == 0:
                    act.wait_ge(s_zs[2], q * 16)
                    act.wait_ge(s_cv, q * 36)
                nc.scalar.activation(squares[j], xs[:, j, :], ACT.Square).then_inc(s_lna, 1)

            def ln_rstd(q):
                act.wait_ge(s_lnm, q * 2 + 2)
                nc.scalar.activation(rstd, p_g[0][:], ACT.Ln, bias=eps_col[:, 0:1]).then_inc(s_lna, 1)

            def exp_rstd(q):
                act.wait_ge(s_lna, q * 8 + 7)
                nc.scalar.activation(rstd, rstd, ACT.Exp, scale=-0.5).then_inc(s_lna, 1)

            def copy_in(q, k):
                t, is_z = in_tile(k)
                act.wait_ge(s_im, q * 12 + k + 1)
                if not is_z:
                    act.wait_ge(s_cv, q * 36 + 6 * (t - 1) if t >= 2 else q * 36 + 0)
                    nc.scalar.activation(xb[:, t % 2, HALO:], p_g[(k + 1) % 2][:], ACT.Identity,
                                         bias=in_b[:, t:t + 1]).then_inc(s_iev, 1)
                else:
                    if t == 0:
                        act.wait_ge(s_lnd, q * 6 + 6)
                    elif t % 2 == 0:
                        act.wait_ge(s_zs[t // 2 - 1], q * 16 + 16)
                    nc.scalar.activation(zt[:, t % 2, :], p_g[(k + 1) % 2][:], ACT.Identity,
                                         bias=in_b[:, ND + t:ND + t + 1]).then_inc(s_iev, 1)

            def silu(q, k):
                for t in (2 * k, 2 * k + 1):
                    act.wait_ge(s_cv, q * 36 + 6 * t + 5)
                    nc.scalar.activation(xc[:, t, :], xc[:, t, :], ACT.Silu, bias=cb[:, t:t + 1]).then_inc(s_si, 1)
                act.wait_ge(s_iev, q * 12 + 4 * k + 4)
                nc.scalar.activation(zt[:], zt[:], ACT.Silu).then_inc(s_si, 1)
                act.preload_act_table_set(EXP_LN)

            def copy_xd(q):
                act.wait_ge(s_xm, q + 1)
                act.wait_ge(s_bcs, q * 16)
                act.wait_ge(s_dtm, q * ND)
                nc.scalar.activation(xd[:], p_g[1][0:64, :], ACT.Copy).then_inc(s_xd, 1)

            def softplus(i, d, step):
                m, r = i * ND + d, d % 2
                if step == 0:
                    act.wait_ge(s_dtm, m + 1)
                    act.wait_ge(s_dt, m * 4)
                    nc.scalar.activation(sp_e[:], p_dt[:], ACT.Abs, bias=dtb[:, d:d + 1]).then_inc(s_jit, 1)
                elif step == 1:
                    act.wait_ge(s_jit, m * 6 + 1 + C_JIT)
                    nc.scalar.activation(sp_e[:], sp_e[:], ACT.Exp, scale=-1.0).then_inc(s_jit, 1)
                elif step == 2:
                    nc.scalar.activation(sp_r[:], p_dt[:], ACT.Relu, bias=dtb[:, d:d + 1]).then_inc(s_jit, 1)
                elif step == 3:
                    act.wait_ge(s_xjl[r], (i * 3 + d // 2 + 1) * 16)
                    act.wait_ge(s_dxu, m)
                    nc.scalar.activation(dx[:], xj[:, r, :], ACT.Copy, scale=dsk[:, d:d + 1]).then_inc(s_jit, 1)
                elif step == 4:
                    act.wait_ge(s_dt, m * 4 + 1)
                    nc.scalar.activation(sp_l[:], sp_w[:], ACT.Ln).then_inc(s_jit, 1)
                else:
                    act.wait_ge(s_re, m + 1)
                    nc.scalar.activation(sp_e[:], sp_e[:], ACT.Square, scale=0.5 ** 0.5).then_inc(s_jit, 1)

            def copy_y(i, d):
                m = i * ND + d
                act.wait_ge(s_hcf, m * NS + C_HCF)
                act.wait_ge(s_yb, m + C_ONE)
                nc.scalar.activation(yt_s[:], p_yt[(d + 1) % 2][:], ACT.Copy).then_inc(s_yts, 1)

            def prepare(q):
                for j in range(NJ):
                    scale(q, j)
                for j in range(NJ):
                    square(q, j)
                ln_rstd(q)
                exp_rstd(q)
                for k in range(12):
                    copy_in(q, k)
                    if k % 4 == 3:
                        silu(q, k // 4)
                copy_xd(q)

            prepare(0)
            for s in range(6):
                softplus(0, 0, s)

            def body(i, kind, b):
                if kind == "image":
                    return
                q = i + 1
                for d in range(ND):
                    m = i * ND + d
                    for n in range(NS):
                        if n == 0:
                            act.wait_ge(s_dt, m * 4 + 4)
                        act.wait_ge(s_scan, m * NS + n - 1 + C_SCAN)
                        nc.scalar.activation(p_da[n % 2][:], dt[:, d % 2, :], ACT.Exp,
                                             scale=neg_a[:, d, n:n + 1]).then_inc(s_exp, 1)
                        if n == 3:
                            copy_y(i, d)
                        if 4 <= n < 10:
                            if d < ND - 1:
                                softplus(i, d + 1, n - 4)
                            else:
                                softplus(q, 0, n - 4)
                        g = d * NS + n
                        if MEAN_AT - 2 < g <= MEAN_AT + 1:
                            scale(q, g - MEAN_AT + 1)
                        if CENTRE_AT + 4 <= g < CENTRE_AT + 7:
                            square(q, g - CENTRE_AT - 4)
                        if g == VAR_AT + 4:
                            ln_rstd(q)
                        if g == VAR_AT + 5:
                            exp_rstd(q)
                        k = g - IN_AT - 4
                        if k % IN_STEP == 0 and 0 <= k // IN_STEP < 12:
                            copy_in(q, k // IN_STEP)
                        k = g - CONV_AT - 14
                        if k % 12 == 0 and 0 <= k // 12 < 3:
                            silu(q, k // 12)
                        if g == X_AT + 7:
                            copy_xd(q)

            chunks(act, body)
            copy_y(NCH, 0)

        @block.vector
        def _(dve):
            dve.sem_inc(s_scan, C_SCAN)
            dve.sem_inc(s_hcv, C_HCV)
            dve.sem_inc(s_res, C_RES)
            dve.sem_inc(s_gate, C_ONE)
            dve.sem_inc(s_state, C_ONE)
            nc.vector.memset(p_yt[1][:], 0.0).then_inc(s_prep, 1)
            nc.vector.memset(zj[:, 1, :], 0.0).then_inc(s_prep, 1)
            nc.vector.memset(yg[:], 0.0).then_inc(s_prep, 1)
            nc.vector.memset(halo[:], 0.0).then_inc(s_prep, 1)
            dve.wait_ge(s_w, 16 * 11)
            dve.wait_ge(s_prepa, 1)
            nc.vector.tensor_scalar(neg_a[:], neg_a[:], -1.0, None, ALU.mult).then_inc(s_prep, 1)
            dve.wait_ge(s_prepm, 1)
            for j in range(NJ):
                nc.vector.tensor_scalar(win[:, j, :], win[:, j, :], lnw[:, j:j + 1], None, ALU.mult)\
                    .then_inc(s_prep, 1)
            dve.wait_ge(s_prep, 8)

            def centre(q, j):
                if j == 0:
                    dve.wait_ge(s_lnm, q * 2 + 1)
                nc.vector.tensor_tensor(xs[:, j, :], xs[:, j, :], p_g[1][:], ALU.subtract).then_inc(s_lnd, 1)

            def normalise(q, j):
                if j == 0:
                    dve.wait_ge(s_lna, q * 8 + 8)
                    dve.wait_ge(s_os, q * 16)
                nc.vector.tensor_tensor(xn[:, j, :], xs[:, j, :], rstd, ALU.mult).then_inc(s_lnd, 1)

            def conv(q, t, step):
                r = t % 2
                base = q * 36 + 6 * t
                if step == 0:
                    dve.wait_ge(s_cv, base)
                    nc.vector.tensor_copy(xb[:, r, 0:HALO], halo[:, t, :]).then_inc(s_cv, 1)
                elif step == 1:
                    dve.wait_ge(s_iev, q * 12 + 4 * (t // 2) + t % 2 + 1)
                    dve.wait_ge(s_cv, base + 1)
                    if t == 0:
                        dve.wait_ge(s_xm, q)
                    if t % 2 == 0:
                        dve.wait_ge(s_xcs[t // 2], q * 16)
                    nc.vector.tensor_scalar(xc[:, t, :], xb[:, r, 0:CH], cw[:, t, 0:1], None, ALU.mult)\
                        .then_inc(s_cv, 1)
                elif step < 5:
                    dve.wait_ge(s_cv, base + step)
                    nc.vector.scalar_tensor_tensor(out=xc[:, t, :], in0=xb[:, r, step - 1:step - 1 + CH],
                                                   scalar=cw[:, t, step - 1:step], in1=xc[:, t, :],
                                                   op0=ALU.mult, op1=ALU.add).then_inc(s_cv, 1)
                else:
                    nc.vector.tensor_copy(halo[:, t, :], xb[:, r, CH:CH + HALO]).then_inc(s_cv, 1)

            def clear_halo(q, b):
                dve.wait_ge(s_cv, q * 36)
                nc.vector.memset(halo[:], 0.0).then_inc(s_prep, 1)
                dve.wait_ge(s_prep, b * 2 + 10)

            def softplus(i, d, step):
                m = i * ND + d
                if step == 0:
                    dve.wait_ge(s_jit, m * 6 + 2 + C_JIT)
                    nc.vector.tensor_scalar(sp_w[:], sp_e[:], 1.0, None, ALU.add).then_inc(s_dt, 1)
                elif step == 1:
                    dve.wait_ge(s_jit, m * 6 + 5 + C_JIT)
                    nc.vector.scalar_tensor_tensor(out=sp_w[:], in0=sp_w[:], scalar=1.0, in1=sp_l[:],
                                                   op0=ALU.subtract, op1=ALU.subtract).then_inc(s_dt, 1)
                elif step == 2:
                    dve.wait_ge(s_dt, m * 4 + 2)
                    dve.wait_ge(s_jit, m * 6 + 6 + C_JIT)
                    nc.vector.scalar_tensor_tensor(out=sp_w[:], in0=sp_w[:], scalar=0.0, in1=sp_e[:],
                                                   op0=ALU.max, op1=ALU.min).then_inc(s_dt, 1)
                else:
                    dve.wait_ge(s_dt, m * 4 + 3)
                    dve.wait_ge(s_exp, m * NS)
                    dve.wait_ge(s_u, m)
                    nc.vector.tensor_tensor(dt[:, d % 2, :], sp_r[:], sp_w[:], ALU.subtract).then_inc(s_dt, 1)

            def gate(i, d):
                m, e, r = i * ND + d, (d - 1) % ND, (d + 1) % 2
                dve.wait_ge(s_yb, m + 1 + C_ONE)
                if d > 0:
                    dve.wait_ge(s_zjl[r], (i * 3 + e // 2 + 1) * 16 + C_ONE)
                else:
                    dve.wait_ge(s_zjl[r], i * (3 * 16) + C_ONE)
                if d == 1:
                    dve.wait_ge(s_om, i * NJ + NJ)
                nc.vector.tensor_tensor(yg[:, e, :], zj[:, r, :], p_yb[:], ALU.mult).then_inc(s_gate, 1)

            def residual(i, j):
                dve.wait_ge(s_om, i * NJ + j + 1)
                if j == 0:
                    dve.wait_ge(s_rl, i * 16 + 16)
                nc.vector.tensor_tensor(xn[:, j, :], xn[:, j, :], p_g[j % 2][:], ALU.add).then_inc(s_res, 1)

            def statistics(i, j):
                dve.wait_ge(s_res, i * NJ + j + 1 + C_RES)
                dve.wait_ge(s_prep, 8)
                nc.vector.bn_stats(stats[:, bass.ds(i * (NJ * 6) + j * 6, 6)], xn[:, j, :]).then_inc(s_stat, 1)

            def scan(i, d, n):
                m, e = i * ND + d, (i * ND + d) * NS + n
                dve.wait_ge(s_exp, e + 1 + C_EXP)
                dve.wait_ge(s_dbx, e + 1 + C_DBX)
                if (n - RH) % NS in BY_DVE:
                    back = BY_DVE.index((n - RH) % NS) + 1 - (NDV if n < RH else 0)
                    dve.wait_ge(s_hcv, m * NDV + back + C_HCV)
                else:
                    dve.wait_ge(s_hcg, m * NPL + BY_POOL.index(n - RH) + 1)
                dve.wait_ge(s_state, m * 4 + n // 4 + C_ONE)
                nc.vector.tensor_tensor_scan(h[:, n % RH, :], p_da[n % 2][:], dbx[:, n % RH, :],
                                             state[:, d, n:n + 1], ALU.mult, ALU.add).then_inc(s_scan, 1)

            def times_c(i, d, n):
                e = (i * ND + d) * NS + n
                dve.wait_ge(s_scan, e + 1 + C_SCAN)
                dve.wait_ge(s_hcf, e + 1)
                if d == 0 and n == min(k for k in BY_DVE if k // 4 == n // 4):
                    dve.wait_ge(s_cl[n // 4], i * 16 + 16)
                nc.vector.tensor_tensor(hc[:, n % RC, :], h[:, n % RH, :], cc[:, n, :], ALU.mult).then_inc(s_hcv, 1)

            def keep_state(i, d, k):
                dve.wait_ge(s_scan, (i * ND + d) * NS + 4 * k + 4 + C_SCAN)
                nc.vector.tensor_copy(state[:, d, 4 * k:4 * k + 4], h[:, :, CH - 1]).then_inc(s_state, 1)

            def prepare(q):
                for j in range(NJ):
                    centre(q, j)
                for j in range(NJ):
                    normalise(q, j)
                for t in range(ND):
                    for s in range(6):
                        conv(q, t, s)

            prepare(0)
            for s in range(4):
                softplus(0, 0, s)

            def body(i, kind, b):
                if kind == "image":
                    dve.wait_ge(s_state, i * (ND * 4) + C_ONE)
                    dve.wait_ge(s_scan, i * (ND * NS) + C_SCAN)
                    nc.vector.memset(state[:], 0.0).then_inc(s_prep, 1)
                    return
                dve.wait_ge(s_prep, b * 2 + 9)
                q = i + 1
                for d in range(ND):
                    for n in range(NS):
                        scan(i, d, n)
                        if n and n - 1 in BY_DVE:
                            times_c(i, d, n - 1)
                        if n % 4 == 3:
                            keep_state(i, d, n // 4)
                        if n == 6:
                            gate(i, d)
                        if n in (5, 8, 9, 10):
                            if d < ND - 1:
                                softplus(i, d + 1, max(n - 7, 0))
                            else:
                                softplus(q, 0, max(n - 7, 0))
                        g = d * NS + n
                        if g in (OUT_AT + 4, OUT_AT + 7, OUT_AT + 11):
                            j = (g - OUT_AT) // 3 - 1
                            residual(i, j)
                            statistics(i, j)
                        if CENTRE_AT <= g < CENTRE_AT + NJ:
                            centre(q, g - CENTRE_AT)
                        if NORM_AT <= g < NORM_AT + NJ:
                            normalise(q, g - NORM_AT)
                        if g == CONV_AT - 1 and kind == "last":
                            clear_halo(q, b)
                        if CONV_AT <= g < CONV_AT + 6 * ND:
                            conv(q, (g - CONV_AT) // 6, (g - CONV_AT) % 6)
                    times_c(i, d, NS - 1)

            chunks(dve, body)
            gate(NCH, 0)
            for j in range(NJ):
                residual(NCH, j)
                statistics(NCH, j)

        @block.gpsimd
        def _(pool):
            pool.sem_inc(s_dbx, C_DBX)
            pool.sem_inc(s_u, C_U)

            def relu_e(i, d):
                m = i * ND + d
                pool.wait_ge(s_jit, m * 6 + 3 + C_JIT)
                nc.gpsimd.tensor_tensor(sp_r[:], sp_r[:], sp_e[:], ALU.add).then_inc(s_re, 1)

            def dt_x(i, d):
                m, r = i * ND + d, d % 2
                pool.wait_ge(s_dt, m * 4 + 4)
                pool.wait_ge(s_xjl[r], (i * 3 + d // 2 + 1) * 16)
                pool.wait_ge(s_dbx, m * NS)
                nc.gpsimd.tensor_tensor(u[:, r, :], dt[:, r, :], xj[:, r, :], ALU.mult).then_inc(s_u, 1)

            def times_b(i, d, n):
                m = i * ND + d
                if n == 0:
                    pool.wait_ge(s_u, m + 1 + C_U)
                if d == 0 and n % 4 == 0:
                    pool.wait_ge(s_bl[n // 4], i * 16 + 16)
                pool.wait_ge(s_scan, m * NS + n + 1)
                nc.gpsimd.tensor_tensor(dbx[:, n % RH, :], u[:, d % 2, :], bb[:, n, :], ALU.mult)\
                    .then_inc(s_dbx, 1)

            def times_c(i, d, n):
                e = (i * ND + d) * NS + n
                pool.wait_ge(s_scan, e + 1 + C_SCAN)
                pool.wait_ge(s_hcf, e + 1)
                if d == 0:
                    pool.wait_ge(s_cl[n // 4], i * 16 + 16)
                nc.gpsimd.tensor_tensor(hc[:, n % RC, :], h[:, n % RH, :], cc[:, n, :], ALU.mult)\
                    .then_inc(s_hcg, 1)

            relu_e(0, 0)
            dt_x(0, 0)

            def body(i, kind, b):
                if kind == "image":
                    return
                for d in range(ND):
                    for n in range(NS):
                        times_b(i, d, n)
                        if n - RH in BY_POOL:
                            times_c(i, d, n - RH)
                        if n == 7:
                            if d < ND - 1:
                                relu_e(i, d + 1)
                            else:
                                relu_e(i + 1, 0)
                        if n == 13:
                            if d < ND - 1:
                                dt_x(i, d + 1)
                            else:
                                dt_x(i + 1, 0)

            chunks(pool, body)

        @block.tensor
        def _(pe):
            pe.sem_inc(s_hcf, C_HCF)
            pe.sem_inc(s_yb, C_ONE)
            pe.wait_ge(s_w, 16 * 11)
            for t in range(2 * ND):
                for j in range(NJ):
                    last = nc.tensor.matmul(p_dt[:, t:t + 1], win[:, j, t * P:(t + 1) * P], lnb[:, j:j + 1],
                                            start=j == 0, stop=j == NJ - 1)
            last.then_inc(s_prepm, 1)
            pe.wait_ge(s_prepa, 2)
            pe.wait_ge(s_prep, 8)

            def mean(q):
                pe.wait_ge(s_lna, q * 8 + 3)
                pe.wait_ge(s_xd, q)
                for j in range(NJ):
                    last = nc.tensor.matmul(p_g[1][:], mean_w[:], xs[:, j, :], start=j == 0, stop=j == NJ - 1)
                last.then_inc(s_lnm, 1)

            def variance(q):
                pe.wait_ge(s_lna, q * 8 + 6)
                pe.wait_ge(s_res, q * NJ + 3)
                for j in range(NJ):
                    last = nc.tensor.matmul(p_g[0][:], mean_w[:], squares[j], start=j == 0, stop=j == NJ - 1)
                last.then_inc(s_lnm, 1)

            def project_in(q, k):
                t, is_z = in_tile(k)
                t += ND * is_z
                if k == 0:
                    pe.wait_ge(s_lnd, q * 6 + 6)
                elif k == 1:
                    pe.wait_ge(s_lna, q * 8 + 7)
                else:
                    pe.wait_ge(s_iev, q * 12 + k - 1)
                for j in range(NJ):
                    last = nc.tensor.matmul(p_g[(k + 1) % 2][:], win[:, j, t * P:(t + 1) * P], xn[:, j, :],
                                            start=j == 0, stop=j == NJ - 1)
                last.then_inc(s_im, 1)

            def project_x(q):
                pe.wait_ge(s_si, q * 9 + 8)
                pe.wait_ge(s_iev, q * 12 + 11)
                for t in range(ND):
                    last = nc.tensor.matmul(p_g[1][0:64, :], wx[:, t, :], xc[:, t, :], start=t == 0, stop=t == ND - 1)
                last.then_inc(s_xm, 1)

            def project_dt(i, d):
                m = i * ND + d
                if d == 0:
                    pe.wait_ge(s_xd, i + 1)
                pe.wait_ge(s_jit, m * 6 - 3 + C_JIT)
                nc.tensor.matmul(p_dt[:], wdt[:, d * P:(d + 1) * P], xd[0:RANK, :], start=True, stop=True)\
                    .then_inc(s_dtm, 1)

            def project_out(i, j, prepares=True):
                if j == 0:
                    pe.wait_ge(s_gate, i * ND + 1 + C_ONE)
                    pe.wait_ge(s_iev, i * 12 + 12)
                elif j == 1 and prepares:
                    pe.wait_ge(s_lnd, i * 6 + 9)
                elif j == 1:
                    pe.wait_ge(s_xd, i + 1)
                else:
                    pe.wait_ge(s_res, i * NJ + 1 + C_RES)
                for t in range(ND):
                    last = nc.tensor.matmul(p_g[j % 2][:], wout[:, t, j, :], yg[:, t, :],
                                            start=t == 0, stop=t == ND - 1)
                last.then_inc(s_om, 1)

            def add_skip(i, d):
                m = i * ND + d
                pe.wait_ge(s_jit, m * 6 + 4 + C_JIT)
                pe.wait_ge(s_yts, m + C_ONE)
                for b in range(NT):
                    last = nc.tensor.matmul(p_yt[d % 2][:, b * P:(b + 1) * P], dx[:, b * P:(b + 1) * P], ident[:],
                                            start=b == 0, stop=False, is_transpose=True, skip_group_check=True)
                last.then_inc(s_dxu, 1)

            def add_state(i, d, n):
                m = i * ND + d
                if n in BY_DVE:
                    pe.wait_ge(s_hcv, m * NDV + BY_DVE.index(n) + 1 + C_HCV)
                else:
                    pe.wait_ge(s_hcg, m * NPL + BY_POOL.index(n) + 1)
                for b in range(NT):
                    last = nc.tensor.matmul(p_yt[d % 2][:, b * P:(b + 1) * P], hc[:, n % RC, b * P:(b + 1) * P],
                                            ident[:], start=False, stop=n == NS - 1, is_transpose=True,
                                            skip_group_check=True)
                last.then_inc(s_hcf, 1)

            def turn_back(i, d):
                m = i * ND + d
                pe.wait_ge(s_yts, m + 1 + C_ONE)
                pe.wait_ge(s_gate, m + C_ONE)
                for b in range(NT):
                    last = nc.tensor.matmul(p_yb[:, b * P:(b + 1) * P], yt_s[:, b * P:(b + 1) * P], ident[:],
                                            start=True, stop=True, is_transpose=True)
                last.then_inc(s_yb, 1)

            def prepare(q):
                mean(q)
                variance(q)
                for k in range(12):
                    project_in(q, k)
                project_x(q)

            prepare(0)
            project_dt(0, 0)

            def body(i, kind, b):
                if kind == "image":
                    return
                q = i + 1
                for d in range(ND):
                    add_skip(i, d)
                    for n in range(NS):
                        g = d * NS + n
                        if n == 4:
                            turn_back(i, d)
                        if g in (OUT_AT, OUT_AT + 3, OUT_AT + 6):
                            project_out(i, (g - OUT_AT) // 3)
                        if g == MEAN_AT:
                            mean(q)
                        if g == VAR_AT:
                            variance(q)
                        k = g - IN_AT
                        if k % IN_STEP == 0 and 0 <= k // IN_STEP < 12:
                            project_in(q, k // IN_STEP)
                        if g == X_AT:
                            project_x(q)
                        if n == 1:
                            if d < ND - 1:
                                project_dt(i, d + 1)
                            else:
                                project_dt(q, 0)
                        add_state(i, d, n)

            chunks(pe, body)
            turn_back(NCH, 0)
            for j in range(NJ):
                project_out(NCH, j, prepares=False)


def attention_layer(nc, x1, w_q, w_k, w_v, w_p, proj_b, out, ident, gsc, gbi):
    with ExitStack() as ctx:
        def sb(name, shape):
            return ctx.enter_context(nc.sbuf_tensor(name, shape, F32))

        def sem(name):
            return ctx.enter_context(nc.semaphore(name))

        def bank(name, shape=(P, 512)):
            return ctx.enter_context(nc.psum_tensor(name, list(shape), F32))

        wq = sb("wq", [P, NJ, NU, P])
        wk = sb("wk", [P, NJ, NU, P])
        wv = sb("wv", [P, NJ, DIM])
        wp = sb("wp", [P, NU, NJ, P])
        pb = sb("pb", [P, NJ])
        x1s = sb("x1s", [P, 2, NJ, CH])
        xn = sb("axn", [P, 2, NJ, CH])
        qs = sb("qs", [P, 2, NU, CH])
        ks = sb("ks", [P, 2, NU, CH])
        vs = sb("vs", [P, 2, 2, NU, HP])
        pr = sb("pr", [P, 2, NU, 2, WIN])
        mx = sb("mx", [P, 2, NU, 2])
        sm = sb("sm", [P, 2, NU, 2])
        ri = sb("ri", [P, 2, NU, 2])
        pt = sb("pt", [P, NU, P])
        ot = sb("ot", [P, 2, NU, CH])
        p_s = [bank("p_s0"), bank("p_s1")]
        p_o = [bank("p_o0"), bank("p_o1")]
        p_t = bank("p_t")
        p_v = bank("p_v")
        p_d = [bank("p_d0"), bank("p_d1")]

        s_w = sem("a_weights")
        s_zero = sem("a_zeroed")
        s_xl = [sem("a_x0"), sem("a_x1")]
        s_rl = [sem("a_residual0"), sem("a_residual1")]
        s_os = [sem("a_out0"), sem("a_out1")]
        s_xn = sem("a_scaled")
        s_qk = sem("a_qk_mm")
        s_qkc = sem("a_qk_copied")
        s_vm = sem("a_v_mm")
        s_vca = sem("a_v_copied_act")
        s_vcd = sem("a_v_copied_dve")
        s_sm = sem("a_scores")
        s_dv = sem("a_softmax")
        s_ex = sem("a_exp")
        s_pt = sem("a_turned")
        s_ptc = sem("a_turned_copied")
        s_om = sem("a_pv")
        s_oc = sem("a_pv_copied")
        s_pm = sem("a_proj")
        s_pd = sem("a_added")
        block = ctx.enter_context(nc.Block())

        def pairs(eng, body):
            with eng.Fori(0, NCH // 2) as half:
                for r in range(2):
                    body(half * 2 + r, half, r)

        @block.sync
        def _(sp):
            for dst, src in ((wq, w_q), (wk, w_k), (wv, w_v), (wp, w_p), (pb, proj_b)):
                sp.dma_start(dst[:], src).then_inc(s_w, 16)
            for s in s_os:
                sp.sem_inc(s, C_ATT)
            for r in range(2):
                sp.dma_start(xn[:, r], x1[r + 1]).then_inc(s_xl[r], 16)
            sp.dma_start(x1s[:, 0], x1[1]).then_inc(s_rl[0], 16)

            def body(g, half, r):
                if r == 0:
                    sp.wait_ge(s_os[1], half * 16 + C_ATT)
                else:
                    sp.wait_ge(s_os[0], half * 16 + 16 + C_ATT)
                sp.dma_start(x1s[:, 1 - r], x1[(g + 1) % NCH + 1]).then_inc(s_rl[1 - r], 16)
                sp.wait_ge(s_vm, g * NT + NT + C_ATT)
                sp.dma_start(xn[:, r], x1[(g + 2) % NCH + 1]).then_inc(s_xl[r], 16)
                sp.wait_ge(s_pd, g * NJ + NJ + C_ATT)
                sp.dma_start(out[g], x1s[:, r]).then_inc(s_os[r], 16)

            pairs(sp, body)
            for r in range(2):
                sp.wait_ge(s_os[r], NCH // 2 * 16 + C_ATT)
                sp.wait_ge(s_xl[r], (NCH // 2 + 1) * 16)
            sp.wait_ge(s_rl[0], (NCH // 2 + 1) * 16)

        @block.scalar
        def _(act):
            act.sem_inc(s_ptc, C_ATT)
            def scale(g, r, loads):
                act.wait_ge(s_xl[r], loads)
                at = bass.ds(g % NCH, 1)
                for j in range(NJ):
                    nc.scalar.activation(xn[:, r, j, :], xn[:, r, j, :], ACT.Identity, scale=gsc[:, at],
                                         bias=gbi[:, at]).then_inc(s_xn, 1)

            def copy_qk(g, r, k):
                act.wait_ge(s_qk, g * 8 + k + 1)
                if k == 0:
                    act.wait_ge(s_sm, g * NT - NT + C_ATT)
                dst = (qs if k < NU else ks)[:, r, k % NU, :]
                nc.scalar.activation(dst, p_d[k % 2][:], ACT.Copy).then_inc(s_qkc, 1)

            def copy_v(g, s):
                w = g * NT + s
                act.wait_ge(s_vm, w + 1 + C_ATT)
                act.wait_ge(s_om, w - 1 + C_ATT)
                for c in range(2):
                    src = p_v[64 * c:64 * c + 64, 0:DIM].rearrange("p (u a e) -> p u a e", a=2, e=HD)
                    nc.scalar.activation(vs[0:64, s % 2, c, :, 0:HD], src[:, :, 0, :], ACT.Copy).then_inc(s_vca, 1)

            def exps(g, s):
                w = g * NT + s
                act.wait_ge(s_dv, w * 7 + 4 + C_ATT)
                nc.scalar.activation(pr[:, s % 2], pr[:, s % 2], ACT.Exp, scale=HD ** -0.5).then_inc(s_ex, 1)

            def copy_t(g, s):
                w = g * NT + s
                act.wait_ge(s_pt, w + 1)
                act.wait_ge(s_om, w + C_ATT)
                nc.scalar.activation(pt[:], p_t[:], ACT.Copy).then_inc(s_ptc, 1)

            act.wait_ge(s_zero, 1)
            scale(0, 0, 16)
            for k in range(8):
                copy_qk(0, 0, k)
            scale(1, 1, 16)
            copy_v(0, 0)

            def body(g, half, r):
                for s in range(NT):
                    if s:
                        copy_v(g, s)
                        copy_t(g, s - 1)
                        exps(g, s)
                        copy_qk(g + 1, 1 - r, 2 * s)
                        if s < NT - 1:
                            copy_qk(g + 1, 1 - r, 2 * s + 1)
                    else:
                        copy_qk(g + 1, 1 - r, 0)
                        exps(g, 0)
                        copy_qk(g + 1, 1 - r, 1)
                copy_t(g, NT - 1)
                copy_qk(g + 1, 1 - r, 7)
                copy_v(g + 1, 0)
                scale(g + 2, r, half * 16 + 32)

            pairs(act, body)

        @block.vector
        def _(dve):
            for s in (s_pd, s_vcd, s_dv, s_oc):
                dve.sem_inc(s, C_ATT)
            nc.vector.memset(vs[:], 0.0).then_inc(s_zero, 1)
            dve.wait_ge(s_zero, 1)
            dve.wait_ge(s_w, 16 * 5)

            def copy_v(g, s):
                w = g * NT + s
                dve.wait_ge(s_vca, w * 2 + 2)
                for c in range(2):
                    src = p_v[64 * c:64 * c + 64, 0:DIM].rearrange("p (u a e) -> p u a e", a=2, e=HD)
                    nc.vector.tensor_copy(vs[64:128, s % 2, c, :, 0:HD], src[:, :, 1, :]).then_inc(s_vcd, 1)

            def maxima(g, s):
                w, r = g * NT + s, s % 2
                dve.wait_ge(s_sm, w + 1 + C_ATT)
                for a in range(2):
                    v = p_s[a][:, 0:NU * WIN].rearrange("p (u k) -> p u k", k=WIN)
                    nc.vector.tensor_reduce(mx[:, r, :, a], v, AX.X, ALU.max).then_inc(s_dv, 1)
                for a in range(2):
                    v = p_s[a][:, 0:NU * WIN].rearrange("p (u k) -> p u k", k=WIN)
                    m = mx[:, r, :, a:a + 1].to_broadcast([P, NU, WIN])
                    dve.wait_ge(s_dv, w * 7 + a + 1 + C_ATT)
                    nc.vector.tensor_tensor(pr[:, r, :, a, :], v, m, ALU.subtract).then_inc(s_dv, 1)

            def normalise(g, s):
                w, r = g * NT + s, s % 2
                dve.wait_ge(s_ex, w + 1)
                nc.vector.tensor_reduce(sm[:, r], pr[:, r], AX.X, ALU.add).then_inc(s_dv, 1)
                dve.wait_ge(s_dv, w * 7 + 5 + C_ATT)
                nc.vector.reciprocal(ri[:, r], sm[:, r]).then_inc(s_dv, 1)
                dve.wait_ge(s_dv, w * 7 + 6 + C_ATT)
                flat = pr[:, r].rearrange("p u a k -> p (u a) k")
                inv = ri[:, r].rearrange("p u (a o) -> p (u a) o", o=1).to_broadcast([P, HEADS, WIN])
                nc.vector.tensor_tensor(flat, flat, inv, ALU.mult).then_inc(s_dv, 1)

            def copy_o(g, r, s):
                w = g * NT + s
                dve.wait_ge(s_om, w + 1 + C_ATT)
                dve.wait_ge(s_pm, g * NJ + C_ATT)
                for a in range(2):
                    v = p_o[a][64 * a:64 * a + 64, :].rearrange("p (u t) -> p u t", t=P)
                    nc.vector.tensor_copy(ot[64 * a:64 * a + 64, r, :, s * P:(s + 1) * P], v).then_inc(s_oc, 1)

            def add(g, half, r, j):
                dve.wait_ge(s_rl[r], half * 16 + 16)
                dve.wait_ge(s_pm, g * NJ + j + 1 + C_ATT)
                nc.vector.scalar_tensor_tensor(out=x1s[:, r, j, :], in0=p_d[j % 2][:], scalar=pb[:, j:j + 1],
                                               in1=x1s[:, r, j, :], op0=ALU.add, op1=ALU.add).then_inc(s_pd, 1)

            copy_v(0, 0)

            def body(g, half, r):
                for s in range(NT):
                    if s:
                        copy_v(g, s)
                    maxima(g, s)
                    if s:
                        copy_o(g, r, s - 1)
                    normalise(g, s)
                copy_o(g, r, NT - 1)
                copy_v(g + 1, 0)
                for j in range(NJ):
                    add(g, half, r, j)

            pairs(dve, body)

        @block.tensor
        def _(pe):
            for s in (s_vm, s_sm, s_om, s_pm):
                pe.sem_inc(s, C_ATT)
            pe.wait_ge(s_w, 16 * 5)
            pe.wait_ge(s_zero, 1)

            def project_qk(g, r, k):
                if k == 0:
                    pe.wait_ge(s_xn, g * NJ + NJ)
                if k < 2:
                    pe.wait_ge(s_pd, g * NJ - NJ + C_ATT)
                else:
                    pe.wait_ge(s_qkc, g * 8 + k - 1)
                w = wq if k < NU else wk
                for j in range(NJ):
                    last = nc.tensor.matmul(p_d[k % 2][:], w[:, j, k % NU, :], xn[:, r, j, :],
                                            start=j == 0, stop=j == NJ - 1)
                last.then_inc(s_qk, 1)

            def values(g, r, s):
                w = g * NT + s
                pe.wait_ge(s_vcd, w * 2 + C_ATT)
                for j in range(NJ):
                    last = nc.tensor.matmul(p_v[:, 0:DIM], xn[:, r, j, s * P:(s + 1) * P], wv[:, j, :],
                                            start=j == 0, stop=j == NJ - 1)
                last.then_inc(s_vm, 1)

            def scores(g, r, s):
                w = g * NT + s
                pe.wait_ge(s_qkc, g * 8 + 8)
                pe.wait_ge(s_dv, w * 7 - 3 + C_ATT)
                nc.tensor.matmul(p_s[0][:, 0:1], ident[:], ident[:, 0:1], start=True, stop=True)
                for a in range(2):
                    for uu in range(NU):
                        for c in range(2):
                            at = slice(s * P + c * WIN, s * P + (c + 1) * WIN)
                            last = nc.tensor.matmul(
                                p_s[a][64 * c:64 * c + 64, uu * WIN:(uu + 1) * WIN],
                                qs[64 * a:64 * a + HD, r, uu, at], ks[64 * a:64 * a + HD, r, uu, at],
                                start=True, stop=True)
                last.then_inc(s_sm, 1)

            def turn(g, s):
                w = g * NT + s
                pe.wait_ge(s_dv, w * 7 + 7 + C_ATT)
                pe.wait_ge(s_ptc, w + C_ATT)
                for uu in range(NU):
                    last = nc.tensor.matmul(p_t[:, uu * P:(uu + 1) * P],
                                            pr[:, s % 2, uu].rearrange("p a k -> p (a k)"), ident[:],
                                            start=True, stop=True, is_transpose=True)
                last.then_inc(s_pt, 1)

            def weigh(g, s):
                w = g * NT + s
                pe.wait_ge(s_ptc, w + 1 + C_ATT)
                pe.wait_ge(s_vca, w * 2 + 2)
                pe.wait_ge(s_vcd, w * 2 + 2 + C_ATT)
                pe.wait_ge(s_oc, w * 2 + C_ATT)
                nc.tensor.matmul(p_o[0][:, 0:1], ident[:], ident[:, 0:1], start=True, stop=True)
                for a in range(2):
                    for uu in range(NU):
                        for c in range(2):
                            at = slice(uu * P + c * WIN, uu * P + (c + 1) * WIN)
                            last = nc.tensor.matmul(
                                p_o[a][64 * a:64 * a + 64, at], vs[64 * a:64 * a + 64, s % 2, c, uu, :],
                                pt[64 * a:64 * a + 64, uu, c * WIN:(c + 1) * WIN], start=True, stop=True)
                last.then_inc(s_om, 1)

            def project(g, r, j):
                if j == 0:
                    pe.wait_ge(s_oc, g * (2 * NT) + 2 * NT + C_ATT)
                if j < 2:
                    pe.wait_ge(s_qkc, g * 8 + 8 + 7 + j)
                else:
                    pe.wait_ge(s_pd, g * NJ + 1 + C_ATT)
                for uu in range(NU):
                    last = nc.tensor.matmul(p_d[j % 2][:], wp[:, uu, j, :], ot[:, r, uu, :],
                                            start=uu == 0, stop=uu == NU - 1)
                last.then_inc(s_pm, 1)

            for k in range(8):
                project_qk(0, 0, k)
            values(0, 0, 0)

            def body(g, half, r):
                for s in range(NT):
                    if s:
                        values(g, r, s)
                    scores(g, r, s)
                    if s:
                        turn(g, s - 1)
                    project_qk(g + 1, 1 - r, 2 * s)
                    if s:
                        weigh(g, s - 1)
                    if s < NT - 1:
                        project_qk(g + 1, 1 - r, 2 * s + 1)
                turn(g, NT - 1)
                project_qk(g + 1, 1 - r, 7)
                weigh(g, NT - 1)
                values(g + 1, 1 - r, 0)
                for j in range(NJ):
                    project(g, r, j)

            pairs(pe, body)


def kernel(**inputs):
    import concourse.bacc as _bacc
    from concourse.bass_utils import run_bass_kernel_spmd as _run

    a = {k.replace("L0_conv_", "").replace("L1_conv_", "a_"): np.asarray(v) for k, v in inputs.items()}

    def slabs(w):
        return w.reshape(P, NJ, *w.shape[1:])

    def tiles(w):
        return np.moveaxis(w.reshape(ND, P, *w.shape[1:]), 0, 1)

    def two_heads(w):
        o = np.zeros((*w.shape[:-1], HEADS, HP), w.dtype)
        o[..., :HD] = w.reshape(*w.shape[:-1], HEADS, HD)
        return o.reshape(*w.shape[:-1], NU, P)

    x = a["x"].reshape(NBATCH, P, NJ, CPB, CH).transpose(0, 3, 1, 2, 4).reshape(NCH, P, NJ, CH)
    wx = np.zeros((DIN, 64), a["x_proj_w"].dtype)
    wx[:, :RANK] = a["x_proj_w"][:RANK].T
    wx[:, 32:] = a["x_proj_w"][RANK:].T
    wo = tiles(a["out_proj_w"].T)
    qkv = a["a_qkv_w"]
    wpt = two_heads(a["a_proj_w"]).reshape(DIM, NU, P)
    laid = {
        "x": x,
        "ln_w": a["ln_w"].reshape(P, NJ),
        "ln_b": a["ln_b"].reshape(P, NJ),
        "w_in": slabs(a["in_proj_w"].T),
        "conv_w": tiles(a["conv_w"].reshape(DIN, HALO + 1)),
        "conv_b": tiles(a["conv_b"]),
        "w_x": tiles(wx),
        "w_dt": a["dt_w"].T,
        "dt_b": tiles(a["dt_b"]),
        "a_log": tiles(a["A_log"]),
        "d_skip": tiles(a["D"]),
        "w_out": wo.reshape(P, ND, P, NJ).transpose(0, 1, 3, 2),
        "w_q": two_heads(slabs(qkv[:DIM].T)),
        "w_k": two_heads(slabs(qkv[DIM:2 * DIM].T)),
        "w_v": slabs(qkv[2 * DIM:].T),
        "w_p": wpt.reshape(P, NJ, NU, P).transpose(3, 2, 1, 0),
        "proj_b": a["a_proj_b"].reshape(P, NJ),
    }
    nc = _bacc.Bacc("TRN2", target_bir_lowering=False, num_devices=1)
    arrays, args = {}, {}
    for name, v in laid.items():
        v = np.ascontiguousarray(v)
        arrays[f"in_{name}"] = v
        args[name] = nc.dram_tensor(f"in_{name}", v.shape, mybir.dt.from_np(v.dtype), kind="ExternalInput").ap()
    out = nc.dram_tensor("out_0", (NCH, P, NJ, CH), F32, kind="ExternalOutput").ap()
    build(nc, out=out, **args)
    r = _run(nc, [arrays], core_ids=[0])
    y = r.results[0]["out_0"]
    return y.reshape(NBATCH, CPB, P, NJ, CH).transpose(0, 2, 3, 1, 4).reshape(a["x"].shape)
```

```python
from contextlib import ExitStack

import numpy as np

import concourse.bass as bass
from concourse import mybir

F32 = mybir.dt.float32
F32R = mybir.dt.float32r
U32 = mybir.dt.uint32
HIGH_BITS = 0xFFFFF000
ALU = mybir.AluOpType
ACT = mybir.ActivationFunctionType
AX = mybir.AxisListType

P = 128
NBATCH, DIM, L = 4, 384, 4096
NJ = DIM // P
CH = 512
CPB = L // CH
NCH = NBATCH * CPB
DIN = 2 * DIM
ND = DIN // P
NS = 16
RANK = DIM // 16
NT = CH // P
HALO = 3
GROUP_PARTS = 4
HEADS, HD, WIN = 8, DIM // 8, 64
HP = 64
NU = HEADS // 2

BY_POOL = (0, 3, 6, 9)
BY_DVE = tuple(n for n in range(NS) if n not in BY_POOL)
NDV, NPL = len(BY_DVE), len(BY_POOL)
SUM_ORDER = [[n] * (n in BY_DVE) + [n - 4] * (n - 4 in BY_POOL) for n in range(NS)]
RH = 4
RV, RG = 6, 2

SCALE_AT, MEAN_AT, CENTRE_AT, SQUARE_AT = 1, 4, 6, 7
OUT_AT, RESIDUAL_AT = (6, 9, 12), (10, 13, 17)
VAR_AT, RSTD_AT, NORM_AT = 18, 24, 26
IN_AT, IN_STEP, COPY_IN_AT, CONV_AT, SILU_AT = 28, 3, 33, 31, 46
X_AT, COPY_X_AT = 69, 77
DT_AT, SOFTPLUS_ACT, SOFTPLUS_DVE, DT_X_AT = 1, (5, 6, 7, 8, 9, 10, 11), (7, 10, 11, 12), 15
COPY_Y_AT, TURN_AT, GATE_AT = 5, 3, 6

EXP_LN = "natural_log_exp_and_others"

C_SCAN, C_HCV, C_DBX, C_EXP, C_U, C_RES, C_JIT, C_ONE = 4, 4, NS, NS, 1, NJ, 12, 1
C_ATT = 8


def build(nc, x, ln_w, ln_b, w_in, conv_w, conv_b, w_x, w_dt, dt_b, a_log, d_skip, w_out,
          w_q, w_k, w_v, w_p, proj_b, out):
    xc_d = nc.dram_tensor("xc_spill", (NCH + 1, P, ND, CH), F32).ap()
    z_d = nc.dram_tensor("z_spill", (NCH + 1, P, ND, CH), F32).ap()
    bc_d = nc.dram_tensor("bc_spill", (NCH + 1, 2 * NS, CH), F32).ap()
    x1_d = nc.dram_tensor("x1", (NCH + 1, P, NJ, CH), F32).ap()
    with ExitStack() as ctx:
        ident = ctx.enter_context(nc.sbuf_tensor("ident", [P, P], F32))
        quarter = ctx.enter_context(nc.sbuf_tensor("quarter", [P, P], F32))
        mean_w = ctx.enter_context(nc.sbuf_tensor("mean_w", [P, P], F32))
        eps_col = ctx.enter_context(nc.sbuf_tensor("eps_col", [P, 1], F32))
        stats = ctx.enter_context(nc.sbuf_tensor("stats", [P, (NCH + 1) * NJ * 6], F32))
        gsc = ctx.enter_context(nc.sbuf_tensor("gsc", [P, NCH], F32))
        gbi = ctx.enter_context(nc.sbuf_tensor("gbi", [P, NCH], F32))
        input_statistics(nc, x, ident, quarter, mean_w, eps_col, stats)
        group_affine(nc, "in", stats, quarter, eps_col, gsc, gbi)
        scan_layer(nc, x, ln_w, ln_b, w_in, conv_w, conv_b, w_x, w_dt, dt_b, a_log, d_skip, w_out,
                   xc_d, z_d, bc_d, x1_d, ident, mean_w, eps_col, stats, gsc, gbi)
        group_affine(nc, "mid", stats, quarter, eps_col, gsc, gbi)
        attention_layer(nc, x1_d, w_q, w_k, w_v, w_p, proj_b, out, ident, gsc, gbi)


def input_statistics(nc, x, ident, quarter, mean_w, eps_col, stats):
    RX = 4
    with ExitStack() as ctx:
        xt = ctx.enter_context(nc.sbuf_tensor("st_x", [P, RX, NJ, CH], F32))
        loaded = [ctx.enter_context(nc.semaphore(f"st_loaded{r}")) for r in range(RX)]
        done = ctx.enter_context(nc.semaphore("st_done"))
        made = ctx.enter_context(nc.semaphore("st_made"))
        block = ctx.enter_context(nc.Block())

        @block.sync
        def _(sp):
            with sp.Fori(0, NCH // RX) as g:
                for r in range(RX):
                    sp.wait_ge(done, g * (RX * NJ) + (r + 1) * NJ)
                    sp.dma_start(xt[:, r], x[g * RX + r]).then_inc(loaded[r], 16)

        @block.vector
        def _(dve):
            dve.sem_inc(done, RX * NJ)
            nc.vector.memset(stats[:, 0:NJ * 6], 0.0)
            nc.vector.memset(eps_col[:], 1e-5)
            nc.vector.memset(mean_w[:], 1.0 / DIM)
            with dve.Fori(0, NCH // RX) as g:
                for r in range(RX):
                    dve.wait_ge(loaded[r], g * 16 + 16)
                    for j in range(NJ):
                        at = (g * RX + (r + 1)) * (NJ * 6) + j * 6
                        nc.vector.bn_stats(stats[:, bass.ds(at, 6)], xt[:, r, j, :]).then_inc(done, 1)

        @block.gpsimd
        def _(pool):
            nc.gpsimd.memset(ident[:], 0.0).then_inc(made, 1)
            nc.gpsimd.memset(quarter[:], 1.0 / GROUP_PARTS).then_inc(made, 1)
            pool.wait_ge(made, 2)
            nc.gpsimd.affine_select(out=ident[:], in_=ident[:], compare_op=ALU.not_equal, fill=1.0,
                                    base=0, pattern=[[-1, P]], channel_multiplier=1).then_inc(made, 1)
            v = quarter[:].rearrange("p (g k) -> p g k", k=GROUP_PARTS)
            nc.gpsimd.affine_select(out=v, in_=v, compare_op=ALU.is_ge, fill=0.0, base=0,
                                    pattern=[[-GROUP_PARTS, P // GROUP_PARTS], [0, GROUP_PARTS]],
                                    channel_multiplier=1).then_inc(made, 1)
            pool.wait_ge(made, 4)
            nc.gpsimd.affine_select(out=v, in_=v, compare_op=ALU.is_ge, fill=0.0, base=GROUP_PARTS - 1,
                                    pattern=[[GROUP_PARTS, P // GROUP_PARTS], [0, GROUP_PARTS]],
                                    channel_multiplier=-1).then_inc(made, 1)
            pool.wait_ge(made, 5)


def group_affine(nc, tag, stats, quarter, eps_col, gsc, gbi):
    with ExitStack() as ctx:
        mv = ctx.enter_context(nc.sbuf_tensor(f"{tag}_mv", [P, NBATCH, 2], F32))
        dev = ctx.enter_context(nc.sbuf_tensor(f"{tag}_dev", [P, NBATCH], F32))
        sq = ctx.enter_context(nc.sbuf_tensor(f"{tag}_sq", [P, NBATCH], F32))
        mean = ctx.enter_context(nc.sbuf_tensor(f"{tag}_mean", [P, NBATCH], F32))
        rs = ctx.enter_context(nc.sbuf_tensor(f"{tag}_rs", [P, NBATCH], F32))
        bi = ctx.enter_context(nc.sbuf_tensor(f"{tag}_bi", [P, NBATCH], F32))
        pm = ctx.enter_context(nc.psum_tensor(f"{tag}_pm", [P, 512], F32))
        pv = ctx.enter_context(nc.psum_tensor(f"{tag}_pv", [P, 512], F32))
        dv = ctx.enter_context(nc.semaphore(f"{tag}_dv"))
        mm = ctx.enter_context(nc.semaphore(f"{tag}_mm"))
        ac = ctx.enter_context(nc.semaphore(f"{tag}_ac"))
        block = ctx.enter_context(nc.Block())

        @block.vector
        def _(dve):
            per = CPB * NJ * 6
            for b in range(NBATCH):
                s = stats[:, NJ * 6 + b * per:NJ * 6 + (b + 1) * per]
                nc.vector.bn_aggr(mv[:, b, :], s).then_inc(dv, 1)
            dve.wait_ge(dv, 4)
            nc.vector.tensor_copy(mean[:], mv[:, :, 0]).then_inc(dv, 1)
            dve.wait_ge(mm, 1)
            nc.vector.tensor_tensor(dev[:], mv[:, :, 0], pm[:, 0:NBATCH], ALU.subtract).then_inc(dv, 1)
            dve.wait_ge(dv, 6)
            nc.vector.tensor_tensor(sq[:], dev[:], dev[:], ALU.mult).then_inc(dv, 1)
            dve.wait_ge(dv, 7)
            nc.vector.tensor_tensor(sq[:], sq[:], mv[:, :, 1], ALU.add).then_inc(dv, 1)
            dve.wait_ge(ac, 2)
            nc.vector.scalar_tensor_tensor(out=bi[:], in0=pm[:, 0:NBATCH], scalar=-1.0, in1=rs[:],
                                           op0=ALU.mult, op1=ALU.mult).then_inc(dv, 1)
            dve.wait_ge(dv, 9)
            for dst, src in ((gsc, rs), (gbi, bi)):
                wide = src[:].rearrange("p (b o) -> p b o", o=1).to_broadcast([P, NBATCH, CPB])
                nc.vector.tensor_copy(dst[:].rearrange("p (b c) -> p b c", c=CPB), wide).then_inc(dv, 1)
            dve.wait_ge(dv, 11)

        @block.tensor
        def _(pe):
            pe.wait_ge(dv, 5)
            nc.tensor.matmul(pm[:, 0:NBATCH], quarter[:], mean[:], start=True, stop=True).then_inc(mm, 1)
            pe.wait_ge(dv, 8)
            nc.tensor.matmul(pv[:, 0:NBATCH], quarter[:], sq[:], start=True, stop=True).then_inc(mm, 1)

        @block.scalar
        def _(act):
            act.preload_act_table_set(EXP_LN)
            act.wait_ge(mm, 2)
            nc.scalar.activation(rs[:], pv[:, 0:NBATCH], ACT.Ln, bias=eps_col[:, 0:1]).then_inc(ac, 1)
            act.wait_ge(ac, 1)
            nc.scalar.activation(rs[:], rs[:], ACT.Exp, scale=-0.5).then_inc(ac, 1)
            act.wait_ge(ac, 2)


def scan_layer(nc, x, ln_w, ln_b, w_in, conv_w, conv_b, w_x, w_dt, dt_b, a_log, d_skip, w_out,
               xc_d, z_d, bc_d, x1_d, ident, mean_w, eps_col, stats, gsc, gbi):
    with ExitStack() as ctx:
        def sb(name, shape):
            return ctx.enter_context(nc.sbuf_tensor(name, shape, F32))

        def sem(name):
            return ctx.enter_context(nc.semaphore(name))

        win = sb("win", [P, NJ, 2 * DIN])
        wx = sb("wx", [P, ND, 64])
        wdt = sb("wdt", [RANK, DIN])
        wout = sb("wout", [P, ND, NJ, P])
        cw = sb("cw", [P, ND, HALO + 1])
        cb = sb("cb", [P, ND])
        dtb = sb("dtb", [P, ND])
        dsk = sb("dsk", [P, ND])
        neg_a = sb("neg_a", [P, ND, NS])
        lnw = sb("lnw", [P, NJ])
        lnb = sb("lnb", [P, NJ])
        in_b = sb("in_b", [P, 2 * ND])
        xs = sb("xs", [P, NJ, CH])
        xn = sb("xn", [P, NJ, CH])
        xb = sb("xb", [P, 2, HALO + CH])
        halo = sb("halo", [P, ND, HALO])
        xc = sb("xc", [P, ND, CH])
        zt = sb("zt", [P, 2, CH])
        rstd = zt[:, 0, :]
        squares = [zt[:, 0, :], zt[:, 1, :], xb[:, 0, 0:CH]]
        xd = sb("xd", [64, CH])
        sp_e = sb("sp_e", [P, CH])
        sp_l = sb("sp_l", [P, CH])
        sp_w = sb("sp_w", [P, CH])
        sp_r = sb("sp_r", [P, CH])
        dt = sb("dt", [P, 2, CH])
        u = sb("u", [P, 2, CH])
        xj = sb("xj", [P, 2, CH])
        zj = sb("zj", [P, 2, CH])
        dx = sb("dx", [P, CH])
        bb = sb("bb", [P, NS, CH])
        cc = sb("cc", [P, NS, CH])
        dbx = sb("dbx", [P, RH, CH])
        h = sb("h", [P, RH, CH])
        hc_v = sb("hc_v", [P, RV, CH])
        hc_g = sb("hc_g", [P, RG, CH])
        state = sb("state", [P, ND, NS])
        yt_s = sb("yt_s", [P, CH])
        yg = sb("yg", [P, ND, CH])

        def bank(name):
            return ctx.enter_context(nc.psum_tensor(name, [P, 512], F32))

        p_da = [bank("p_da0"), bank("p_da1")]
        p_yt = [bank("p_yt0"), bank("p_yt1")]
        p_yb = bank("p_yb")
        p_dt = bank("p_dt")
        p_g = [bank("p_g0"), bank("p_g1")]

        s_w = sem("weights_loaded")
        s_prep = sem("prepared")
        s_prepa = sem("prepared_act")
        s_prepm = sem("prepared_pe")
        s_exp = sem("exp_done")
        s_scan = sem("scan_done")
        s_hcv = sem("hc_dve")
        s_hcg = sem("hc_pool")
        s_hvf = sem("hc_dve_used")
        s_hgf = sem("hc_pool_used")
        s_state = sem("state_kept")
        s_dbx = sem("dbx_done")
        s_u = sem("u_done")
        s_jit = sem("softplus_act")
        s_dt = sem("softplus_dve")
        s_dtm = sem("dt_mm")
        s_dxu = sem("dx_used")
        s_yts = sem("yt_copied")
        s_yb = sem("yb_done")
        s_gate = sem("gated")
        s_om = sem("out_mm")
        s_res = sem("residual_done")
        s_stat = sem("stats_done")
        s_lna = sem("ln_act")
        s_lnm = sem("ln_mm")
        s_lnd = sem("ln_dve")
        s_im = sem("in_mm")
        s_iev = sem("in_copied")
        s_cv0 = sem("conv_begun")
        s_cv = sem("conv_done")
        s_si = sem("silu_done")
        s_xm = sem("x_mm")
        s_xd = sem("xd_done")
        s_rl = sem("residual_loaded")
        s_xl = sem("x_loaded")
        s_os = sem("x1_stored")
        s_xcs = [sem(f"xc_stored{k}") for k in range(3)]
        s_zs = [sem(f"z_stored{k}") for k in range(3)]
        s_bcs = sem("bc_stored")
        s_bl = [sem(f"b_loaded{q}") for q in range(4)]
        s_cl = [sem(f"c_loaded{q}") for q in range(4)]
        s_xjl = [sem("xj_loaded0"), sem("xj_loaded1")]
        s_zjl = [sem("zj_loaded0"), sem("zj_loaded1")]

        block = ctx.enter_context(nc.Block())

        def in_tile(k):
            return 2 * (k // 4) + k % 2, k % 4 >= 2

        def chunks(eng, body):
            with eng.Fori(0, NBATCH) as b:
                body(b * CPB, "image", b)
                with eng.Fori(0, CPB - 1) as c:
                    body(b * CPB + c, "chunk", b)
                body(b * CPB + (CPB - 1), "last", b)

        @block.sync
        def _(sp):
            sp.dma_start(xs[:], x[0]).then_inc(s_xl, 16)
            for dst, src in ((win, w_in), (wx, w_x), (wdt, w_dt), (wout, w_out), (cw, conv_w), (cb, conv_b),
                             (dtb, dt_b), (dsk, d_skip), (neg_a, a_log), (lnw, ln_w), (lnb, ln_b)):
                sp.dma_start(dst[:], src).then_inc(s_w, 16)
            for s in s_zjl:
                sp.sem_inc(s, C_ONE)

            def load_x(q, at):
                sp.wait_ge(s_lnd, q * 6)
                sp.dma_start(xs[:], x[at]).then_inc(s_xl, 16)

            def store_silu(q, k):
                sp.wait_ge(s_si, q * 9 + 3 * k + 3)
                sp.dma_start(xc_d[q, :, 2 * k:2 * k + 2, :], xc[:, 2 * k:2 * k + 2, :]).then_inc(s_xcs[k], 16)
                sp.dma_start(z_d[q, :, 2 * k:2 * k + 2, :], zt[:]).then_inc(s_zs[k], 16)

            def store_bc(q):
                sp.wait_ge(s_xd, q + 1)
                sp.dma_start(bc_d[q], xd[32:64, :]).then_inc(s_bcs, 16)

            def load_b(q, k):
                src = bc_d[q, 4 * k:4 * k + 4, :].rearrange("(o n) t -> o n t", o=1).to_broadcast([P, 4, CH])
                sp.dma_start(bb[:, 4 * k:4 * k + 4, :], src).then_inc(s_bl[k], 16)

            def load_c(q, k):
                src = bc_d[q, NS + 4 * k:NS + 4 * k + 4, :].rearrange("(o n) t -> o n t", o=1).to_broadcast([P, 4, CH])
                sp.dma_start(cc[:, 4 * k:4 * k + 4, :], src).then_inc(s_cl[k], 16)

            def load_xj(i, d):
                m, r = i * ND + d, d % 2
                sp.compute_val(m * 7 - 8 + C_JIT)
                sp.compute_val(m)
                sp.compute_val(i * 16 + 16)
                sp.wait_ge(s_jit, m * 7 - 8 + C_JIT)
                sp.wait_ge(s_u, m)
                if d % 2 == 0:
                    sp.wait_ge(s_xcs[d // 2], i * 16 + 16)
                sp.dma_start(xj[:, r, :], xc_d[i, :, d, :]).then_inc(s_xjl[r], 16)

            def load_zj(i, d):
                m, r = i * ND + d, d % 2
                sp.compute_val(m + C_ONE)
                sp.compute_val(i * 16 + 16)
                sp.wait_ge(s_gate, m + C_ONE)
                if d % 2 == 0:
                    sp.wait_ge(s_zs[d // 2], i * 16 + 16)
                sp.dma_start(zj[:, r, :], z_d[i, :, d, :]).then_inc(s_zjl[r], 16)

            load_x(1, 1)
            for k in range(3):
                store_silu(0, k)
            sp.wait_ge(s_xcs[0], 16)
            sp.wait_ge(s_zs[0], 16)
            sp.dma_start(xj[:, 0, :], xc_d[0, :, 0, :]).then_inc(s_xjl[0], 16)
            sp.dma_start(zj[:, 0, :], z_d[0, :, 0, :]).then_inc(s_zjl[0], 16)
            store_bc(0)
            sp.wait_ge(s_bcs, 16)
            for k in range(4):
                load_b(0, k)
                load_c(0, k)

            def body(i, kind, b):
                if kind == "image":
                    return
                q = i + 1
                for d in range(ND):
                    if d < ND - 1:
                        load_xj(i, d + 1)
                    else:
                        load_xj(q, 0)
                    if d == 0:
                        sp.wait_ge(s_im, i * 12 + 12)
                        sp.dma_start(xn[:], x[(i + (NCH - 1)) % NCH]).then_inc(s_rl, 16)
                    if d == 1:
                        sp.wait_ge(s_stat, i * NJ + NJ)
                        sp.dma_start(x1_d[i], xn[:]).then_inc(s_os, 16)
                    if d == 2:
                        load_x(q + 1, (q + 1) % NCH)
                    if d < ND - 1:
                        load_zj(i, d + 1)
                    if 2 <= d < 5:
                        store_silu(q, d - 2)
                    if d == 5:
                        store_bc(q)
                        load_zj(q, 0)
                        sp.wait_ge(s_bcs, q * 16 + 16)
                        for k in range(4):
                            e = i * (ND * NS) + 5 * NS + 4 * k + 4
                            sp.wait_ge(s_dbx, e + C_DBX)
                            load_b(q, k)
                            v = i * (ND * NDV) + 5 * NDV + sum(n < 4 * k + 4 for n in BY_DVE) + C_HCV
                            g = i * (ND * NPL) + 5 * NPL + sum(n < 4 * k + 4 for n in BY_POOL)
                            sp.compute_val(v)
                            sp.compute_val(g)
                            sp.wait_ge(s_hcv, v)
                            sp.wait_ge(s_hcg, g)
                            load_c(q, k)

            chunks(sp, body)
            sp.wait_ge(s_im, NCH * 12 + 12)
            sp.dma_start(xn[:], x[NCH - 1]).then_inc(s_rl, 16)
            sp.wait_ge(s_stat, NCH * NJ + NJ)
            sp.dma_start(x1_d[NCH], xn[:]).then_inc(s_os, 16)
            sp.wait_ge(s_xl, (NCH + 2) * 16)
            sp.wait_ge(s_os, (NCH + 1) * 16)
            for s in s_xcs + s_zs + s_bl + s_cl:
                sp.wait_ge(s, (NCH + 1) * 16)
            sp.wait_ge(s_xjl[0], (NCH * 3 + 1) * 16)
            sp.wait_ge(s_zjl[0], (NCH * 3 + 1) * 16 + C_ONE)

        @block.scalar
        def _(act):
            act.sem_inc(s_exp, C_EXP)
            act.sem_inc(s_jit, C_JIT)
            act.sem_inc(s_yts, C_ONE)
            act.preload_act_table_set(EXP_LN)
            def scale(q, j):
                if j == 0:
                    act.wait_ge(s_xl, q * 16 + 16)
                at = bass.ds(q % NCH, 1)
                nc.scalar.activation(xs[:, j, :], xs[:, j, :], ACT.Identity, scale=gsc[:, at],
                                     bias=gbi[:, at]).then_inc(s_lna, 1)

            def square(q, j):
                act.wait_ge(s_lnd, q * 6 + j + 1)
                if j == 0:
                    act.wait_ge(s_zs[2], q * 16)
                    act.wait_ge(s_cv, q * 30)
                nc.scalar.activation(squares[j], xs[:, j, :], ACT.Square).then_inc(s_lna, 1)

            def ln_rstd(q):
                act.wait_ge(s_lnm, q * 2 + 2)
                nc.scalar.activation(rstd, p_g[0][:], ACT.Ln, bias=eps_col[:, 0:1]).then_inc(s_lna, 1)

            def exp_rstd(q):
                act.wait_ge(s_lna, q * 8 + 7)
                nc.scalar.activation(rstd, rstd, ACT.Exp, scale=-0.5).then_inc(s_lna, 1)

            def copy_in(q, k):
                t, is_z = in_tile(k)
                act.wait_ge(s_im, q * 12 + k + 1)
                if not is_z:
                    act.wait_ge(s_cv, q * 30 + 5 * max(t - 1, 0))
                    nc.scalar.activation(xb[:, t % 2, HALO:], p_g[(k + 1) % 2][:], ACT.Identity,
                                         bias=in_b[:, t:t + 1]).then_inc(s_iev, 1)
                    if t == 0:
                        act.wait_ge(s_xm, q)
                    if t % 2 == 0:
                        act.wait_ge(s_xcs[t // 2], q * 16)
                    act.wait_ge(s_iev, q * 12 + k + 1)
                    nc.scalar.activation(xc[:, t, :], xb[:, t % 2, HALO:], ACT.Copy,
                                         scale=cw[:, t, HALO:HALO + 1]).then_inc(s_cv0, 1)
                else:
                    if t == 0:
                        act.wait_ge(s_lnd, q * 6 + 6)
                    elif t % 2 == 0:
                        act.wait_ge(s_zs[t // 2 - 1], q * 16 + 16)
                    nc.scalar.activation(zt[:, t % 2, :], p_g[(k + 1) % 2][:], ACT.Identity,
                                         bias=in_b[:, ND + t:ND + t + 1]).then_inc(s_iev, 1)

            def silu(q, k):
                for t in (2 * k, 2 * k + 1):
                    act.wait_ge(s_cv, q * 30 + 5 * t + 4)
                    nc.scalar.activation(xc[:, t, :], xc[:, t, :], ACT.Silu, bias=cb[:, t:t + 1]).then_inc(s_si, 1)
                act.wait_ge(s_iev, q * 12 + 4 * k + 4)
                nc.scalar.activation(zt[:], zt[:], ACT.Silu).then_inc(s_si, 1)
                act.preload_act_table_set(EXP_LN)

            def copy_xd(q):
                act.wait_ge(s_xm, q + 1)
                act.wait_ge(s_bcs, q * 16)
                act.wait_ge(s_dtm, q * ND)
                nc.scalar.activation(xd[:], p_g[1][0:64, :], ACT.Copy).then_inc(s_xd, 1)

            def softplus(i, d, step):
                m, r = i * ND + d, d % 2
                if step == 0:
                    act.wait_ge(s_dtm, m + 1)
                    act.wait_ge(s_dt, m * 4)
                    nc.scalar.activation(sp_e[:], p_dt[:], ACT.Abs, bias=dtb[:, d:d + 1]).then_inc(s_jit, 1)
                elif step == 1:
                    act.wait_ge(s_jit, m * 7 + 1 + C_JIT)
                    nc.scalar.activation(sp_e[:], sp_e[:], ACT.Exp, scale=-1.0).then_inc(s_jit, 1)
                elif step == 2:
                    nc.scalar.activation(sp_r[:], p_dt[:], ACT.Relu, bias=dtb[:, d:d + 1]).then_inc(s_jit, 1)
                elif step == 3:
                    act.wait_ge(s_jit, m * 7 + 2 + C_JIT)
                    nc.scalar.activation(sp_w[:], sp_e[:], ACT.Identity, bias=1.0).then_inc(s_jit, 1)
                elif step == 4:
                    act.wait_ge(s_jit, m * 7 + 4 + C_JIT)
                    nc.scalar.activation(sp_l[:], sp_w[:], ACT.Ln).then_inc(s_jit, 1)
                elif step == 5:
                    act.wait_ge(s_xjl[r], (i * 3 + d // 2 + 1) * 16)
                    act.wait_ge(s_dxu, m)
                    nc.scalar.activation(dx[:], xj[:, r, :], ACT.Copy, scale=dsk[:, d:d + 1]).then_inc(s_jit, 1)
                else:
                    act.wait_ge(s_dt, m * 4 + 1)
                    nc.scalar.activation(sp_e[:], sp_e[:], ACT.Square, scale=0.5 ** 0.5).then_inc(s_jit, 1)

            def copy_y(i, d):
                m = i * ND + d
                act.wait_ge(s_hvf, m * NDV + RV)
                act.wait_ge(s_hgf, m * NPL + RG)
                act.wait_ge(s_yb, m + C_ONE)
                nc.scalar.activation(yt_s[:], p_yt[(d + 1) % 2][:], ACT.Copy).then_inc(s_yts, 1)

            for j in range(NJ):
                scale(0, j)
            act.wait_ge(s_w, 16 * 11)
            nc.scalar.activation(neg_a[:], neg_a[:], ACT.Exp).then_inc(s_prepa, 1)
            for j in range(NJ):
                square(0, j)
            act.wait_ge(s_prepm, 1)
            nc.scalar.activation(in_b[:], p_dt[:, 0:2 * ND], ACT.Copy).then_inc(s_prepa, 1)
            ln_rstd(0)
            exp_rstd(0)
            act.wait_ge(s_prepa, 2)
            act.wait_ge(s_prep, 8)
            for k in range(12):
                copy_in(0, k)
                if k % 4 == 3:
                    silu(0, k // 4)
            copy_xd(0)
            for s in range(7):
                softplus(0, 0, s)

            def body(i, kind, b):
                if kind == "image":
                    return
                q = i + 1
                for d in range(ND):
                    m = i * ND + d
                    for n in range(NS):
                        if n == 0:
                            act.wait_ge(s_dt, m * 4 + 4)
                        act.wait_ge(s_scan, m * NS + n - 1 + C_SCAN)
                        nc.scalar.activation(p_da[n % 2][:], dt[:, d % 2, :], ACT.Exp,
                                             scale=neg_a[:, d, n:n + 1]).then_inc(s_exp, 1)
                        if n == COPY_Y_AT:
                            copy_y(i, d)
                        if n in SOFTPLUS_ACT:
                            softplus(*((i, d + 1) if d < ND - 1 else (q, 0)), SOFTPLUS_ACT.index(n))
                        g = d * NS + n
                        if SCALE_AT <= g < SCALE_AT + NJ:
                            scale(q, g - SCALE_AT)
                        if SQUARE_AT <= g < SQUARE_AT + NJ:
                            square(q, g - SQUARE_AT)
                        if g == RSTD_AT:
                            ln_rstd(q)
                        if g == RSTD_AT + 1:
                            exp_rstd(q)
                        k = g - COPY_IN_AT
                        if k % IN_STEP == 0 and 0 <= k // IN_STEP < 12:
                            copy_in(q, k // IN_STEP)
                        k = g - SILU_AT
                        if k % (4 * IN_STEP) == 0 and 0 <= k // (4 * IN_STEP) < 3:
                            silu(q, k // (4 * IN_STEP))
                        if g == COPY_X_AT:
                            copy_xd(q)

            chunks(act, body)
            copy_y(NCH, 0)

        @block.vector
        def _(dve):
            dve.sem_inc(s_scan, C_SCAN)
            dve.sem_inc(s_hcv, C_HCV)
            dve.sem_inc(s_res, C_RES)
            dve.sem_inc(s_gate, C_ONE)
            dve.sem_inc(s_state, C_ONE)
            nc.vector.memset(p_yt[1][:], 0.0).then_inc(s_prep, 1)
            nc.vector.memset(zj[:, 1, :], 0.0).then_inc(s_prep, 1)
            nc.vector.memset(yg[:], 0.0).then_inc(s_prep, 1)
            nc.vector.memset(halo[:], 0.0).then_inc(s_prep, 1)

            def centre(q, j):
                if j == 0:
                    dve.wait_ge(s_lnm, q * 2 + 1)
                nc.vector.tensor_tensor(xs[:, j, :], xs[:, j, :], p_g[1][:], ALU.subtract).then_inc(s_lnd, 1)

            def normalise(q, j):
                if j == 0:
                    dve.wait_ge(s_lna, q * 8 + 8)
                    dve.wait_ge(s_os, q * 16)
                nc.vector.tensor_tensor(xn[:, j, :], xs[:, j, :], rstd, ALU.mult).then_inc(s_lnd, 1)

            def conv(q, t, step):
                r = t % 2
                base = q * 30 + 5 * t
                if step == 0:
                    dve.wait_ge(s_cv, base)
                    nc.vector.tensor_copy(xb[:, r, 0:HALO], halo[:, t, :]).then_inc(s_cv, 1)
                elif step <= HALO:
                    if step == 1:
                        dve.wait_ge(s_cv0, q * ND + t + 1)
                    dve.wait_ge(s_cv, base + step)
                    nc.vector.scalar_tensor_tensor(out=xc[:, t, :], in0=xb[:, r, step - 1:step - 1 + CH],
                                                   scalar=cw[:, t, step - 1:step], in1=xc[:, t, :],
                                                   op0=ALU.mult, op1=ALU.add).then_inc(s_cv, 1)
                else:
                    nc.vector.tensor_copy(halo[:, t, :], xb[:, r, CH:CH + HALO]).then_inc(s_cv, 1)

            def clear_halo(q, b):
                dve.wait_ge(s_cv, q * 30)
                nc.vector.memset(halo[:], 0.0).then_inc(s_prep, 1)
                dve.wait_ge(s_prep, b * 2 + 10)

            def softplus(i, d, step):
                m = i * ND + d
                if step == 0:
                    dve.wait_ge(s_jit, m * 7 + 3 + C_JIT)
                    nc.vector.tensor_tensor(sp_r[:], sp_r[:], sp_e[:], ALU.add).then_inc(s_dt, 1)
                elif step == 1:
                    dve.wait_ge(s_jit, m * 7 + 5 + C_JIT)
                    nc.vector.scalar_tensor_tensor(out=sp_w[:], in0=sp_w[:], scalar=1.0, in1=sp_l[:],
                                                   op0=ALU.subtract, op1=ALU.subtract).then_inc(s_dt, 1)
                elif step == 2:
                    dve.wait_ge(s_dt, m * 4 + 2)
                    dve.wait_ge(s_jit, m * 7 + 7 + C_JIT)
                    nc.vector.scalar_tensor_tensor(out=sp_w[:], in0=sp_w[:], scalar=0.0, in1=sp_e[:],
                                                   op0=ALU.max, op1=ALU.min).then_inc(s_dt, 1)
                else:
                    dve.wait_ge(s_dt, m * 4 + 3)
                    dve.wait_ge(s_exp, m * NS)
                    dve.wait_ge(s_u, m)
                    nc.vector.tensor_tensor(dt[:, d % 2, :], sp_r[:], sp_w[:], ALU.subtract).then_inc(s_dt, 1)

            def gate(i, d):
                m, e, r = i * ND + d, (d - 1) % ND, (d + 1) % 2
                dve.wait_ge(s_yb, m + 1 + C_ONE)
                if d > 0:
                    dve.wait_ge(s_zjl[r], (i * 3 + e // 2 + 1) * 16 + C_ONE)
                else:
                    dve.wait_ge(s_zjl[r], i * (3 * 16) + C_ONE)
                if d == 1:
                    dve.wait_ge(s_om, i * NJ + NJ)
                nc.vector.tensor_tensor(yg[:, e, :], zj[:, r, :], p_yb[:], ALU.mult).then_inc(s_gate, 1)

            def residual(i, j):
                dve.wait_ge(s_om, i * NJ + j + 1)
                if j == 0:
                    dve.wait_ge(s_rl, i * 16 + 16)
                nc.vector.tensor_tensor(xn[:, j, :], xn[:, j, :], p_g[j % 2][:], ALU.add).then_inc(s_res, 1)

            def statistics(i, j):
                dve.wait_ge(s_res, i * NJ + j + 1 + C_RES)
                dve.wait_ge(s_prep, 8)
                nc.vector.bn_stats(stats[:, bass.ds(i * (NJ * 6) + j * 6, 6)], xn[:, j, :]).then_inc(s_stat, 1)

            def scan(i, d, n):
                m, e = i * ND + d, (i * ND + d) * NS + n
                dve.wait_ge(s_exp, e + 1 + C_EXP)
                dve.wait_ge(s_dbx, e + 1 + C_DBX)
                if (n - RH) % NS in BY_DVE:
                    back = BY_DVE.index((n - RH) % NS) + 1 - (NDV if n < RH else 0)
                    dve.wait_ge(s_hcv, m * NDV + back + C_HCV)
                else:
                    dve.wait_ge(s_hcg, m * NPL + BY_POOL.index(n - RH) + 1)
                dve.wait_ge(s_state, m * 4 + n // 4 + C_ONE)
                nc.vector.tensor_tensor_scan(h[:, n % RH, :], p_da[n % 2][:], dbx[:, n % RH, :],
                                             state[:, d, n:n + 1], ALU.mult, ALU.add).then_inc(s_scan, 1)

            def times_c(i, d, n):
                m, k = i * ND + d, BY_DVE.index(n)
                dve.wait_ge(s_scan, m * NS + n + 1 + C_SCAN)
                dve.wait_ge(s_hvf, m * NDV + k + 1)
                if d == 0 and n == min(k for k in BY_DVE if k // 4 == n // 4):
                    dve.wait_ge(s_cl[n // 4], i * 16 + 16)
                nc.vector.tensor_tensor(hc_v[:, k % RV, :], h[:, n % RH, :], cc[:, n, :], ALU.mult).then_inc(s_hcv, 1)

            def keep_state(i, d, k):
                dve.wait_ge(s_scan, (i * ND + d) * NS + 4 * k + 4 + C_SCAN)
                nc.vector.tensor_copy(state[:, d, 4 * k:4 * k + 4], h[:, :, CH - 1]).then_inc(s_state, 1)

            for j in range(NJ):
                centre(0, j)
            dve.wait_ge(s_w, 16 * 11)
            dve.wait_ge(s_prepa, 1)
            nc.vector.tensor_scalar(neg_a[:], neg_a[:], -1.0, None, ALU.mult).then_inc(s_prep, 1)
            dve.wait_ge(s_prepm, 1)
            for j in range(NJ):
                nc.vector.tensor_scalar(win[:, j, :], win[:, j, :], lnw[:, j:j + 1], None, ALU.mult)\
                    .then_inc(s_prep, 1)
            dve.wait_ge(s_prep, 8)
            for j in range(NJ):
                normalise(0, j)
            for t in range(ND):
                for s in range(5):
                    conv(0, t, s)
            for s in range(4):
                softplus(0, 0, s)

            def body(i, kind, b):
                if kind == "image":
                    dve.wait_ge(s_state, i * (ND * 4) + C_ONE)
                    dve.wait_ge(s_scan, i * (ND * NS) + C_SCAN)
                    nc.vector.memset(state[:], 0.0).then_inc(s_prep, 1)
                    return
                dve.wait_ge(s_prep, b * 2 + 9)
                q = i + 1
                for d in range(ND):
                    for n in range(NS):
                        scan(i, d, n)
                        if n and n - 1 in BY_DVE:
                            times_c(i, d, n - 1)
                        if n % 4 == 3:
                            keep_state(i, d, n // 4)
                        if n == GATE_AT:
                            gate(i, d)
                        if n in SOFTPLUS_DVE:
                            softplus(*((i, d + 1) if d < ND - 1 else (q, 0)), SOFTPLUS_DVE.index(n))
                        g = d * NS + n
                        if g in RESIDUAL_AT:
                            residual(i, RESIDUAL_AT.index(g))
                            statistics(i, RESIDUAL_AT.index(g))
                        if CENTRE_AT <= g < CENTRE_AT + NJ:
                            centre(q, g - CENTRE_AT)
                        if NORM_AT <= g < NORM_AT + NJ:
                            normalise(q, g - NORM_AT)
                        if g == CONV_AT - 1 and kind == "last":
                            clear_halo(q, b)
                        if CONV_AT <= g < CONV_AT + 6 * ND and (g - CONV_AT) % 6 < 5:
                            conv(q, (g - CONV_AT) // 6, (g - CONV_AT) % 6)
                    times_c(i, d, NS - 1)

            chunks(dve, body)
            gate(NCH, 0)
            for j in range(NJ):
                residual(NCH, j)
                statistics(NCH, j)

        @block.gpsimd
        def _(pool):
            pool.sem_inc(s_dbx, C_DBX)
            pool.sem_inc(s_u, C_U)

            def dt_x(i, d):
                m, r = i * ND + d, d % 2
                pool.wait_ge(s_dt, m * 4 + 4)
                pool.wait_ge(s_xjl[r], (i * 3 + d // 2 + 1) * 16)
                pool.wait_ge(s_dbx, m * NS)
                nc.gpsimd.tensor_tensor(u[:, r, :], dt[:, r, :], xj[:, r, :], ALU.mult).then_inc(s_u, 1)

            def times_b(i, d, n):
                m = i * ND + d
                if n == 0:
                    pool.wait_ge(s_u, m + 1 + C_U)
                if d == 0 and n % 4 == 0:
                    pool.wait_ge(s_bl[n // 4], i * 16 + 16)
                pool.wait_ge(s_scan, m * NS + n + 1)
                nc.gpsimd.tensor_tensor(dbx[:, n % RH, :], u[:, d % 2, :], bb[:, n, :], ALU.mult)\
                    .then_inc(s_dbx, 1)

            def times_c(i, d, n):
                m, k = i * ND + d, BY_POOL.index(n)
                pool.wait_ge(s_scan, m * NS + n + 1 + C_SCAN)
                pool.wait_ge(s_hgf, m * NPL + k + 1)
                if d == 0:
                    pool.wait_ge(s_cl[n // 4], i * 16 + 16)
                nc.gpsimd.tensor_tensor(hc_g[:, k % RG, :], h[:, n % RH, :], cc[:, n, :], ALU.mult)\
                    .then_inc(s_hcg, 1)

            dt_x(0, 0)

            def body(i, kind, b):
                if kind == "image":
                    return
                for d in range(ND):
                    for n in range(NS):
                        times_b(i, d, n)
                        if n - RH in BY_POOL:
                            times_c(i, d, n - RH)
                        if n == DT_X_AT:
                            dt_x(*((i, d + 1) if d < ND - 1 else (i + 1, 0)))

            chunks(pool, body)

        @block.tensor
        def _(pe):
            pe.sem_inc(s_hvf, RV)
            pe.sem_inc(s_hgf, RG)
            pe.sem_inc(s_yb, C_ONE)

            def mean(q):
                pe.wait_ge(s_lna, q * 8 + 3)
                pe.wait_ge(s_xd, q)
                for j in range(NJ):
                    last = nc.tensor.matmul(p_g[1][:], mean_w[:], xs[:, j, :], start=j == 0, stop=j == NJ - 1)
                last.then_inc(s_lnm, 1)

            def variance(q):
                pe.wait_ge(s_lna, q * 8 + 6)
                pe.wait_ge(s_res, q * NJ + 3)
                for j in range(NJ):
                    last = nc.tensor.matmul(p_g[0][:], mean_w[:], squares[j], start=j == 0, stop=j == NJ - 1)
                last.then_inc(s_lnm, 1)

            def project_in(q, k):
                t, is_z = in_tile(k)
                t += ND * is_z
                if k == 0:
                    pe.wait_ge(s_lnd, q * 6 + 6)
                elif k == 1:
                    pe.wait_ge(s_lna, q * 8 + 7)
                else:
                    pe.wait_ge(s_iev, q * 12 + k - 1)
                for j in range(NJ):
                    last = nc.tensor.matmul(p_g[(k + 1) % 2][:], win[:, j, t * P:(t + 1) * P], xn[:, j, :],
                                            start=j == 0, stop=j == NJ - 1)
                last.then_inc(s_im, 1)

            def project_x(q):
                pe.wait_ge(s_si, q * 9 + 8)
                pe.wait_ge(s_iev, q * 12 + 11)
                for t in range(ND):
                    last = nc.tensor.matmul(p_g[1][0:64, :], wx[:, t, :], xc[:, t, :], start=t == 0, stop=t == ND - 1)
                last.then_inc(s_xm, 1)

            def project_dt(i, d):
                m = i * ND + d
                if d == 0:
                    pe.wait_ge(s_xd, i + 1)
                pe.wait_ge(s_jit, m * 7 - 4 + C_JIT)
                nc.tensor.matmul(p_dt[:], wdt[:, d * P:(d + 1) * P], xd[0:RANK, :], start=True, stop=True)\
                    .then_inc(s_dtm, 1)

            def project_out(i, j, prepares=True):
                if j == 0:
                    pe.wait_ge(s_gate, i * ND + 1 + C_ONE)
                    pe.wait_ge(s_iev, i * 12 + 12)
                elif j == 1 and prepares:
                    pe.wait_ge(s_lnd, i * 6 + 9)
                elif j == 1:
                    pe.wait_ge(s_xd, i + 1)
                else:
                    pe.wait_ge(s_res, i * NJ + 1 + C_RES)
                for t in range(ND):
                    last = nc.tensor.matmul(p_g[j % 2][:], wout[:, t, j, :], yg[:, t, :],
                                            start=t == 0, stop=t == ND - 1)
                last.then_inc(s_om, 1)

            def add_skip(i, d):
                m = i * ND + d
                pe.wait_ge(s_jit, m * 7 + 6 + C_JIT)
                pe.wait_ge(s_yts, m + C_ONE)
                for b in range(NT):
                    last = nc.tensor.matmul(p_yt[d % 2][:, b * P:(b + 1) * P], dx[:, b * P:(b + 1) * P], ident[:],
                                            start=b == 0, stop=False, is_transpose=True, skip_group_check=True)
                last.then_inc(s_dxu, 1)

            def add_state(i, d, n):
                m = i * ND + d
                if n in BY_DVE:
                    k = BY_DVE.index(n)
                    pe.wait_ge(s_hcv, m * NDV + k + 1 + C_HCV)
                    product, used = hc_v[:, k % RV, :], s_hvf
                else:
                    k = BY_POOL.index(n)
                    pe.wait_ge(s_hcg, m * NPL + k + 1)
                    product, used = hc_g[:, k % RG, :], s_hgf
                for b in range(NT):
                    last = nc.tensor.matmul(p_yt[d % 2][:, b * P:(b + 1) * P], product[:, b * P:(b + 1) * P],
                                            ident[:], start=False, stop=n == SUM_ORDER[-1][-1],
                                            is_transpose=True, skip_group_check=True)
                last.then_inc(used, 1)

            def turn_back(i, d):
                m = i * ND + d
                pe.wait_ge(s_yts, m + 1 + C_ONE)
                pe.wait_ge(s_gate, m + C_ONE)
                for b in range(NT):
                    last = nc.tensor.matmul(p_yb[:, b * P:(b + 1) * P], yt_s[:, b * P:(b + 1) * P], ident[:],
                                            start=True, stop=True, is_transpose=True)
                last.then_inc(s_yb, 1)

            mean(0)
            pe.wait_ge(s_w, 16 * 11)
            for t in range(2 * ND):
                for j in range(NJ):
                    last = nc.tensor.matmul(p_dt[:, t:t + 1], win[:, j, t * P:(t + 1) * P], lnb[:, j:j + 1],
                                            start=j == 0, stop=j == NJ - 1)
            last.then_inc(s_prepm, 1)
            variance(0)
            pe.wait_ge(s_prepa, 2)
            pe.wait_ge(s_prep, 8)
            for k in range(12):
                project_in(0, k)
            project_x(0)
            project_dt(0, 0)

            def body(i, kind, b):
                if kind == "image":
                    return
                q = i + 1
                for d in range(ND):
                    add_skip(i, d)
                    for n in range(NS):
                        g = d * NS + n
                        if n == TURN_AT:
                            turn_back(i, d)
                        if g in OUT_AT:
                            project_out(i, OUT_AT.index(g))
                        if g == MEAN_AT:
                            mean(q)
                        if g == VAR_AT:
                            variance(q)
                        k = g - IN_AT
                        if k % IN_STEP == 0 and 0 <= k // IN_STEP < 12:
                            project_in(q, k // IN_STEP)
                        if g == X_AT:
                            project_x(q)
                        if n == DT_AT:
                            if d < ND - 1:
                                project_dt(i, d + 1)
                            else:
                                project_dt(q, 0)
                        for k in SUM_ORDER[n]:
                            add_state(i, d, k)

            chunks(pe, body)
            turn_back(NCH, 0)
            for j in range(NJ):
                project_out(NCH, j, prepares=False)


def attention_layer(nc, x1, w_q, w_k, w_v, w_p, proj_b, out, ident, gsc, gbi):
    with ExitStack() as ctx:
        def sb(name, shape):
            return ctx.enter_context(nc.sbuf_tensor(name, shape, F32))

        def sem(name):
            return ctx.enter_context(nc.semaphore(name))

        def bank(name, shape=(P, 512)):
            return ctx.enter_context(nc.psum_tensor(name, list(shape), F32))

        wq = sb("wq", [P, NJ, NU, P])
        wk = sb("wk", [P, NJ, NU, P])
        wv = sb("wv", [P, NJ, DIM])
        wp = sb("wp", [P, NU, NJ, P])
        pb = sb("pb", [P, NJ])
        split = {}
        for name, like in (("wq", wq), ("wk", wk), ("wv", wv)):
            split[name] = [ctx.enter_context(nc.sbuf_tensor(f"{name}_{part}", list(like.shape), kind))
                           for part, kind in (("high", F32R), ("low", F32R), ("upper", F32))]
        xu = sb("x_upper", [P, 2, NJ, CH])
        xh = ctx.enter_context(nc.sbuf_tensor("x_high", [P, 2, NJ, CH], F32R))
        xl = ctx.enter_context(nc.sbuf_tensor("x_low", [P, 2, NJ, CH], F32R))
        x1s = sb("x1s", [P, 2, NJ, CH])
        xn = sb("axn", [P, 2, NJ, CH])
        qs = sb("qs", [P, 2, NU, CH])
        ks = sb("ks", [P, 2, NU, CH])
        vs = sb("vs", [P, 2, 2, NU, HP])
        pr = sb("pr", [P, 2, NU, 2, WIN])
        mx = sb("mx", [P, 2, NU, 2])
        sm = sb("sm", [P, 2, NU, 2])
        ri = sb("ri", [P, 2, NU, 2])
        pt = sb("pt", [P, NU, P])
        ot = sb("ot", [P, 2, NU, CH])
        p_s = [bank("p_s0"), bank("p_s1")]
        p_o = [bank("p_o0"), bank("p_o1")]
        p_t = bank("p_t")
        p_v = bank("p_v")
        p_d = [bank("p_d0"), bank("p_d1")]

        s_w = sem("a_weights")
        s_zero = sem("a_zeroed")
        s_xl = [sem("a_x0"), sem("a_x1")]
        s_rl = [sem("a_residual0"), sem("a_residual1")]
        s_os = [sem("a_out0"), sem("a_out1")]
        s_xn = sem("a_scaled")
        s_xu = sem("a_x_upper")
        s_xh = sem("a_x_high")
        s_xlo = sem("a_x_low")
        s_wu = sem("a_w_upper")
        s_wh = sem("a_w_high")
        s_wlo = sem("a_w_low")
        s_qk = sem("a_qk_mm")
        s_qkc = sem("a_qk_copied")
        s_vm = sem("a_v_mm")
        s_vca = sem("a_v_copied_act")
        s_vcd = sem("a_v_copied_dve")
        s_sm = sem("a_scores")
        s_dv = sem("a_softmax")
        s_ex = sem("a_exp")
        s_pt = sem("a_turned")
        s_ptc = sem("a_turned_copied")
        s_om = sem("a_pv")
        s_oc = sem("a_pv_copied")
        s_pm = sem("a_proj")
        s_pd = sem("a_added")
        block = ctx.enter_context(nc.Block())

        QK_AT = ((0, 1), (2, 3), (4,), (5, 6))

        def pairs(eng, body):
            with eng.Fori(0, NCH // 2) as half:
                for r in range(2):
                    body(half * 2 + r, half, r)

        @block.sync
        def _(sp):
            for dst, src in ((wq, w_q), (wk, w_k), (wv, w_v), (wp, w_p), (pb, proj_b)):
                sp.dma_start(dst[:], src).then_inc(s_w, 16)
            for s in s_os:
                sp.sem_inc(s, C_ATT)
            for r in range(2):
                sp.dma_start(xn[:, r], x1[r + 1]).then_inc(s_xl[r], 16)
            sp.dma_start(x1s[:, 0], x1[1]).then_inc(s_rl[0], 16)

            def body(g, half, r):
                if r == 0:
                    sp.wait_ge(s_os[1], half * 16 + C_ATT)
                else:
                    sp.wait_ge(s_os[0], half * 16 + 16 + C_ATT)
                sp.dma_start(x1s[:, 1 - r], x1[(g + 1) % NCH + 1]).then_inc(s_rl[1 - r], 16)
                sp.wait_ge(s_xlo, g * NJ + NJ)
                sp.dma_start(xn[:, r], x1[(g + 2) % NCH + 1]).then_inc(s_xl[r], 16)
                sp.wait_ge(s_pd, g * NJ + NJ + C_ATT)
                sp.dma_start(out[g], x1s[:, r]).then_inc(s_os[r], 16)

            pairs(sp, body)
            for r in range(2):
                sp.wait_ge(s_os[r], NCH // 2 * 16 + C_ATT)
                sp.wait_ge(s_xl[r], (NCH // 2 + 1) * 16)
            sp.wait_ge(s_rl[0], (NCH // 2 + 1) * 16)

        @block.scalar
        def _(act):
            act.sem_inc(s_ptc, C_ATT)
            def scale(g, r, loads):
                act.wait_ge(s_xl[r], loads)
                at = bass.ds(g % NCH, 1)
                for j in range(NJ):
                    nc.scalar.activation(xn[:, r, j, :], xn[:, r, j, :], ACT.Identity, scale=gsc[:, at],
                                         bias=gbi[:, at]).then_inc(s_xn, 1)

            def high_part(g, r):
                act.wait_ge(s_vm, g * NT - NT + C_ATT)
                for j in range(NJ):
                    act.wait_ge(s_xu, g * NJ + j + 1)
                    nc.scalar.activation(xh[:, r, j, :], xu[:, r, j, :], ACT.Copy).then_inc(s_xh, 1)

            def copy_qk(g, r, k):
                act.wait_ge(s_qk, g * 8 + k + 1)
                if k == 0:
                    act.wait_ge(s_sm, g * NT - NT + C_ATT)
                dst = (qs if k < NU else ks)[:, r, k % NU, :]
                nc.scalar.activation(dst, p_d[k % 2][:], ACT.Copy).then_inc(s_qkc, 1)

            def copy_v(g, s):
                w = g * NT + s
                act.wait_ge(s_vm, w + 1 + C_ATT)
                act.wait_ge(s_om, w - 1 + C_ATT)
                for c in range(2):
                    src = p_v[64 * c:64 * c + 64, 0:DIM].rearrange("p (u a e) -> p u a e", a=2, e=HD)
                    nc.scalar.activation(vs[0:64, s % 2, c, :, 0:HD], src[:, :, 0, :], ACT.Copy).then_inc(s_vca, 1)

            def exps(g, s):
                w = g * NT + s
                act.wait_ge(s_dv, w * 7 + 4 + C_ATT)
                nc.scalar.activation(pr[:, s % 2], pr[:, s % 2], ACT.Exp, scale=HD ** -0.5).then_inc(s_ex, 1)

            def copy_t(g, s):
                w = g * NT + s
                act.wait_ge(s_pt, w + 1)
                act.wait_ge(s_om, w + C_ATT)
                nc.scalar.activation(pt[:], p_t[:], ACT.Copy).then_inc(s_ptc, 1)

            act.wait_ge(s_zero, 1)
            for k, name in enumerate(("wq", "wk", "wv")):
                act.wait_ge(s_wu, k + 1)
                nc.scalar.activation(split[name][0][:], split[name][2][:], ACT.Copy).then_inc(s_wh, 1)
            scale(0, 0, 16)
            scale(1, 1, 16)
            high_part(0, 0)
            high_part(1, 1)
            for k in range(8):
                copy_qk(0, 0, k)
            copy_v(0, 0)

            def body(g, half, r):
                for s in range(NT):
                    if s:
                        copy_v(g, s)
                        copy_t(g, s - 1)
                        exps(g, s)
                        if s == NT - 1:
                            scale(g + 2, r, half * 16 + 32)
                        for k in QK_AT[s]:
                            copy_qk(g + 1, 1 - r, k)
                    else:
                        copy_qk(g + 1, 1 - r, 0)
                        exps(g, 0)
                        copy_qk(g + 1, 1 - r, 1)
                copy_t(g, NT - 1)
                copy_qk(g + 1, 1 - r, 7)
                copy_v(g + 1, 0)
                high_part(g + 2, r)

            pairs(act, body)

        @block.vector
        def _(dve):
            for s in (s_pd, s_vcd, s_dv, s_oc):
                dve.sem_inc(s, C_ATT)
            nc.vector.memset(vs[:], 0.0).then_inc(s_zero, 1)
            dve.wait_ge(s_zero, 1)
            dve.wait_ge(s_w, 16 * 5)

            def copy_v(g, s):
                w = g * NT + s
                dve.wait_ge(s_vca, w * 2 + 2)
                for c in range(2):
                    src = p_v[64 * c:64 * c + 64, 0:DIM].rearrange("p (u a e) -> p u a e", a=2, e=HD)
                    nc.vector.tensor_copy(vs[64:128, s % 2, c, :, 0:HD], src[:, :, 1, :]).then_inc(s_vcd, 1)

            def maxima(g, s):
                w, r = g * NT + s, s % 2
                dve.wait_ge(s_sm, w + 1 + C_ATT)
                for a in range(2):
                    v = p_s[a][:, 0:NU * WIN].rearrange("p (u k) -> p u k", k=WIN)
                    nc.vector.tensor_reduce(mx[:, r, :, a], v, AX.X, ALU.max).then_inc(s_dv, 1)
                for a in range(2):
                    v = p_s[a][:, 0:NU * WIN].rearrange("p (u k) -> p u k", k=WIN)
                    m = mx[:, r, :, a:a + 1].to_broadcast([P, NU, WIN])
                    dve.wait_ge(s_dv, w * 7 + a + 1 + C_ATT)
                    nc.vector.tensor_tensor(pr[:, r, :, a, :], v, m, ALU.subtract).then_inc(s_dv, 1)

            def normalise(g, s):
                w, r = g * NT + s, s % 2
                dve.wait_ge(s_ex, w + 1)
                nc.vector.tensor_reduce(sm[:, r], pr[:, r], AX.X, ALU.add).then_inc(s_dv, 1)
                dve.wait_ge(s_dv, w * 7 + 5 + C_ATT)
                nc.vector.reciprocal(ri[:, r], sm[:, r]).then_inc(s_dv, 1)
                dve.wait_ge(s_dv, w * 7 + 6 + C_ATT)
                flat = pr[:, r].rearrange("p u a k -> p (u a) k")
                inv = ri[:, r].rearrange("p u (a o) -> p (u a) o", o=1).to_broadcast([P, HEADS, WIN])
                nc.vector.tensor_tensor(flat, flat, inv, ALU.mult).then_inc(s_dv, 1)

            def copy_o(g, r, s):
                w = g * NT + s
                dve.wait_ge(s_om, w + 1 + C_ATT)
                dve.wait_ge(s_pm, g * NJ + C_ATT)
                for a in range(2):
                    v = p_o[a][64 * a:64 * a + 64, :].rearrange("p (u t) -> p u t", t=P)
                    nc.vector.tensor_copy(ot[64 * a:64 * a + 64, r, :, s * P:(s + 1) * P], v).then_inc(s_oc, 1)

            def add(g, half, r, j):
                dve.wait_ge(s_rl[r], half * 16 + 16)
                dve.wait_ge(s_pm, g * NJ + j + 1 + C_ATT)
                nc.vector.scalar_tensor_tensor(out=x1s[:, r, j, :], in0=p_d[j % 2][:], scalar=pb[:, j:j + 1],
                                               in1=x1s[:, r, j, :], op0=ALU.add, op1=ALU.add).then_inc(s_pd, 1)

            def upper_bits(g, r):
                for j in range(NJ):
                    dve.wait_ge(s_xn, g * NJ + j + 1)
                    nc.vector.tensor_scalar(xu[:, r, j, :].bitcast(U32), xn[:, r, j, :].bitcast(U32),
                                            HIGH_BITS, None, ALU.bitwise_and).then_inc(s_xu, 1)

            for name, w in (("wq", wq), ("wk", wk), ("wv", wv)):
                nc.vector.tensor_scalar(split[name][2][:].bitcast(U32), w[:].bitcast(U32), HIGH_BITS, None,
                                        ALU.bitwise_and).then_inc(s_wu, 1)
            upper_bits(0, 0)
            upper_bits(1, 1)
            copy_v(0, 0)

            def body(g, half, r):
                for s in range(NT):
                    if s:
                        copy_v(g, s)
                    maxima(g, s)
                    if s:
                        copy_o(g, r, s - 1)
                    normalise(g, s)
                upper_bits(g + 2, r)
                copy_o(g, r, NT - 1)
                copy_v(g + 1, 0)
                for j in range(NJ):
                    add(g, half, r, j)

            pairs(dve, body)

        @block.gpsimd
        def _(pool):
            for k, (name, w) in enumerate((("wq", wq), ("wk", wk), ("wv", wv))):
                pool.wait_ge(s_wu, k + 1)
                nc.gpsimd.tensor_tensor(split[name][1][:], w[:], split[name][2][:], ALU.subtract)\
                    .then_inc(s_wlo, 1)

            def low_part(g, r):
                pool.wait_ge(s_vm, g * NT - NT + C_ATT)
                for j in range(NJ):
                    pool.wait_ge(s_xu, g * NJ + j + 1)
                    nc.gpsimd.tensor_tensor(xl[:, r, j, :], xn[:, r, j, :], xu[:, r, j, :], ALU.subtract)\
                        .then_inc(s_xlo, 1)

            low_part(0, 0)
            low_part(1, 1)
            pairs(pool, lambda g, half, r: low_part(g + 2, r))

        @block.tensor
        def _(pe):
            for s in (s_vm, s_sm, s_om, s_pm):
                pe.sem_inc(s, C_ATT)
            pe.wait_ge(s_w, 16 * 5)
            pe.wait_ge(s_zero, 1)

            def project_qk(g, r, k):
                if k == 0:
                    pe.wait_ge(s_xlo, g * NJ + NJ)
                    pe.wait_ge(s_xh, g * NJ + NJ)
                if k < 2:
                    pe.wait_ge(s_pd, g * NJ - NJ + C_ATT)
                else:
                    pe.wait_ge(s_qkc, g * 8 + k - 1)
                wh, wl, _ = split["wq" if k < NU else "wk"]
                for j in range(NJ):
                    for n, (w, v) in enumerate(((wh, xh), (wh, xl), (wl, xh))):
                        last = nc.tensor.matmul(p_d[k % 2][:], w[:, j, k % NU, :], v[:, r, j, :],
                                                start=j + n == 0, stop=j + n == NJ + 1)
                last.then_inc(s_qk, 1)

            def values(g, r, s):
                w = g * NT + s
                pe.wait_ge(s_vcd, w * 2 + C_ATT)
                wh, wl, _ = split["wv"]
                for j in range(NJ):
                    for n, (v, w) in enumerate(((xh, wh), (xh, wl), (xl, wh))):
                        last = nc.tensor.matmul(p_v[:, 0:DIM], v[:, r, j, s * P:(s + 1) * P], w[:, j, :],
                                                start=j + n == 0, stop=j + n == NJ + 1)
                last.then_inc(s_vm, 1)

            def scores(g, r, s):
                w = g * NT + s
                pe.wait_ge(s_qkc, g * 8 + 8)
                pe.wait_ge(s_dv, w * 7 - 3 + C_ATT)
                nc.tensor.matmul(p_s[0][:, 0:1], ident[:], ident[:, 0:1], start=True, stop=True)
                for a in range(2):
                    for uu in range(NU):
                        for c in range(2):
                            at = slice(s * P + c * WIN, s * P + (c + 1) * WIN)
                            last = nc.tensor.matmul(
                                p_s[a][64 * c:64 * c + 64, uu * WIN:(uu + 1) * WIN],
                                qs[64 * a:64 * a + HD, r, uu, at], ks[64 * a:64 * a + HD, r, uu, at],
                                start=True, stop=True)
                last.then_inc(s_sm, 1)

            def turn(g, s):
                w = g * NT + s
                pe.wait_ge(s_dv, w * 7 + 7 + C_ATT)
                pe.wait_ge(s_ptc, w + C_ATT)
                for uu in range(NU):
                    last = nc.tensor.matmul(p_t[:, uu * P:(uu + 1) * P],
                                            pr[:, s % 2, uu].rearrange("p a k -> p (a k)"), ident[:],
                                            start=True, stop=True, is_transpose=True)
                last.then_inc(s_pt, 1)

            def weigh(g, s):
                w = g * NT + s
                pe.wait_ge(s_ptc, w + 1 + C_ATT)
                pe.wait_ge(s_vca, w * 2 + 2)
                pe.wait_ge(s_vcd, w * 2 + 2 + C_ATT)
                pe.wait_ge(s_oc, w * 2 + C_ATT)
                nc.tensor.matmul(p_o[0][:, 0:1], ident[:], ident[:, 0:1], start=True, stop=True)
                for a in range(2):
                    for uu in range(NU):
                        for c in range(2):
                            at = slice(uu * P + c * WIN, uu * P + (c + 1) * WIN)
                            last = nc.tensor.matmul(
                                p_o[a][64 * a:64 * a + 64, at], vs[64 * a:64 * a + 64, s % 2, c, uu, :],
                                pt[64 * a:64 * a + 64, uu, c * WIN:(c + 1) * WIN], start=True, stop=True)
                last.then_inc(s_om, 1)

            def project(g, r, j):
                if j == 0:
                    pe.wait_ge(s_oc, g * (2 * NT) + 2 * NT + C_ATT)
                if j < 2:
                    pe.wait_ge(s_qkc, g * 8 + 8 + 7 + j)
                else:
                    pe.wait_ge(s_pd, g * NJ + 1 + C_ATT)
                for uu in range(NU):
                    last = nc.tensor.matmul(p_d[j % 2][:], wp[:, uu, j, :], ot[:, r, uu, :],
                                            start=uu == 0, stop=uu == NU - 1)
                last.then_inc(s_pm, 1)

            pe.wait_ge(s_wlo, 3)
            pe.wait_ge(s_wh, 3)
            for k in range(8):
                project_qk(0, 0, k)
            values(0, 0, 0)

            def body(g, half, r):
                for s in range(NT):
                    if s:
                        values(g, r, s)
                    scores(g, r, s)
                    if s:
                        turn(g, s - 1)
                    first, *rest = QK_AT[s]
                    project_qk(g + 1, 1 - r, first)
                    if s:
                        weigh(g, s - 1)
                    for k in rest:
                        project_qk(g + 1, 1 - r, k)
                turn(g, NT - 1)
                project_qk(g + 1, 1 - r, 7)
                weigh(g, NT - 1)
                values(g + 1, 1 - r, 0)
                for j in range(NJ):
                    project(g, r, j)

            pairs(pe, body)


def kernel(**inputs):
    import concourse.bacc as _bacc
    from concourse.bass_utils import run_bass_kernel_spmd as _run

    a = {k.replace("L0_conv_", "").replace("L1_conv_", "a_"): np.asarray(v) for k, v in inputs.items()}

    def slabs(w):
        return w.reshape(P, NJ, *w.shape[1:])

    def tiles(w):
        return np.moveaxis(w.reshape(ND, P, *w.shape[1:]), 0, 1)

    def two_heads(w):
        o = np.zeros((*w.shape[:-1], HEADS, HP), w.dtype)
        o[..., :HD] = w.reshape(*w.shape[:-1], HEADS, HD)
        return o.reshape(*w.shape[:-1], NU, P)

    x = a["x"].reshape(NBATCH, P, NJ, CPB, CH).transpose(0, 3, 1, 2, 4).reshape(NCH, P, NJ, CH)
    wx = np.zeros((DIN, 64), a["x_proj_w"].dtype)
    wx[:, :RANK] = a["x_proj_w"][:RANK].T
    wx[:, 32:] = a["x_proj_w"][RANK:].T
    wo = tiles(a["out_proj_w"].T)
    qkv = a["a_qkv_w"]
    wpt = two_heads(a["a_proj_w"]).reshape(DIM, NU, P)
    laid = {
        "x": x,
        "ln_w": a["ln_w"].reshape(P, NJ),
        "ln_b": a["ln_b"].reshape(P, NJ),
        "w_in": slabs(a["in_proj_w"].T),
        "conv_w": tiles(a["conv_w"].reshape(DIN, HALO + 1)),
        "conv_b": tiles(a["conv_b"]),
        "w_x": tiles(wx),
        "w_dt": a["dt_w"].T,
        "dt_b": tiles(a["dt_b"]),
        "a_log": tiles(a["A_log"]),
        "d_skip": tiles(a["D"]),
        "w_out": wo.reshape(P, ND, P, NJ).transpose(0, 1, 3, 2),
        "w_q": two_heads(slabs(qkv[:DIM].T)),
        "w_k": two_heads(slabs(qkv[DIM:2 * DIM].T)),
        "w_v": slabs(qkv[2 * DIM:].T),
        "w_p": wpt.reshape(P, NJ, NU, P).transpose(3, 2, 1, 0),
        "proj_b": a["a_proj_b"].reshape(P, NJ),
    }
    nc = _bacc.Bacc("TRN2", target_bir_lowering=False, num_devices=1)
    arrays, args = {}, {}
    for name, v in laid.items():
        v = np.ascontiguousarray(v)
        arrays[f"in_{name}"] = v
        args[name] = nc.dram_tensor(f"in_{name}", v.shape, mybir.dt.from_np(v.dtype), kind="ExternalInput").ap()
    out = nc.dram_tensor("out_0", (NCH, P, NJ, CH), F32, kind="ExternalOutput").ap()
    build(nc, out=out, **args)
    r = _run(nc, [arrays], core_ids=[0])
    y = r.results[0]["out_0"]
    return y.reshape(NBATCH, CPB, P, NJ, CH).transpose(0, 2, 3, 1, 4).reshape(a["x"].shape)
```
